# Optimizing a Trainium2 kernel written in Bass

```python
import numpy as np
import jax
import jax.numpy as jnp

def _softmax(x, axis=-1):
    return jax.nn.softmax(x, axis=axis)

def _gelu(x):
    return jax.nn.gelu(x, approximate=True)

def _silu(x):
    return jax.nn.silu(x)

def _sigmoid(x):
    return jax.nn.sigmoid(x)

def _layernorm(x, axis=-1, eps=1e-05):
    m = jnp.mean(x, axis=axis, keepdims=True)
    v = jnp.var(x, axis=axis, keepdims=True)
    return (x - m) / jnp.sqrt(v + eps)

def _scatter_add(tgt, idx, src, axis=0):
    return tgt.at[idx].add(src)

def _segment_sum(src, seg, n):
    return jax.ops.segment_sum(src, seg, n)
kernel_name = 'mk_seq_postln_d1_jaxref_r8_7190a7'

def setup_inputs(seed: int=0):
    np.random.seed(seed)
    _w = jnp.asarray

    def _L0_attn_setup():
        import jax, jax.numpy as jnp
        import numpy as np
        B, T, C, H = (2, 256, 128, 16)
        R = 32
        LORA_SCALE = 0.5
        HD = C // H

        def lora_linear(x, w, b, la, lb):
            return x @ w.T + b + LORA_SCALE * (x @ la.T @ lb.T)
        key = jax.random.key(seed)
        ks = jax.random.split(key, 8)
        std = 0.02
        return {'x': jax.random.normal(ks[0], (B, T, C), jnp.float32), 'w_attn': jax.random.normal(ks[1], (3 * C, C), jnp.float32) * std, 'b_attn': jnp.zeros((3 * C,), jnp.float32), 'la_attn': jax.random.normal(ks[2], (R, C), jnp.float32) * std, 'lb_attn': jax.random.normal(ks[3], (3 * C, R), jnp.float32) * std, 'w_proj': jax.random.normal(ks[4], (C, C), jnp.float32) * std, 'b_proj': jnp.zeros((C,), jnp.float32), 'la_proj': jax.random.normal(ks[5], (R, C), jnp.float32) * std, 'lb_proj': jax.random.normal(ks[6], (C, R), jnp.float32) * std}
    _L0_attn_in = _L0_attn_setup()

    def _L0_ffn_setup():
        import jax, jax.numpy as jnp
        import numpy as np
        NUM_EXPERTS = 8
        TOP_K = 2
        B, T, D, F = (4, 256, 128, 352)
        key = jax.random.key(seed)
        ks = jax.random.split(key, 5)
        return {'x': jax.random.normal(ks[0], (B, T, D), dtype=jnp.float32), 'router_w': jax.random.normal(ks[1], (D, NUM_EXPERTS), dtype=jnp.float32) * 0.02, 'gate_proj': jax.random.normal(ks[2], (NUM_EXPERTS, D, F), dtype=jnp.float32) * 0.02, 'up_proj': jax.random.normal(ks[3], (NUM_EXPERTS, D, F), dtype=jnp.float32) * 0.02, 'down_proj': jax.random.normal(ks[4], (NUM_EXPERTS, F, D), dtype=jnp.float32) * 0.02}
    _L0_ffn_in = _L0_ffn_setup()
    _d = {'L0_attn_x': _L0_attn_in['x'], 'L0_attn_w_attn': _L0_attn_in['w_attn'], 'L0_attn_b_attn': _L0_attn_in['b_attn'], 'L0_attn_la_attn': _L0_attn_in['la_attn'], 'L0_attn_lb_attn': _L0_attn_in['lb_attn'], 'L0_attn_w_proj': _L0_attn_in['w_proj'], 'L0_attn_b_proj': _L0_attn_in['b_proj'], 'L0_attn_la_proj': _L0_attn_in['la_proj'], 'L0_attn_lb_proj': _L0_attn_in['lb_proj'], 'L0_ffn_router_w': _L0_ffn_in['router_w'], 'L0_ffn_gate_proj': _L0_ffn_in['gate_proj'], 'L0_ffn_up_proj': _L0_ffn_in['up_proj'], 'L0_ffn_down_proj': _L0_ffn_in['down_proj']}
    _x0 = _d['L0_attn_x']
    _d['L0_attn_x'] = jax.random.normal(jax.random.fold_in(jax.random.key(seed), 1), (4, 512, 128), dtype=_x0.dtype)
    del _x0
    return _d

def reference(L0_attn_x, L0_attn_w_attn, L0_attn_b_attn, L0_attn_la_attn, L0_attn_lb_attn, L0_attn_w_proj, L0_attn_b_proj, L0_attn_la_proj, L0_attn_lb_proj, L0_ffn_router_w, L0_ffn_gate_proj, L0_ffn_up_proj, L0_ffn_down_proj):

    def _L0_attn_ref(x, w_attn, b_attn, la_attn, lb_attn, w_proj, b_proj, la_proj, lb_proj):
        import jax, jax.numpy as jnp
        import numpy as np
        B, T, C, H = (2, 256, 128, 16)
        R = 32
        LORA_SCALE = 0.5
        HD = C // H

        def lora_linear(x, w, b, la, lb):
            return x @ w.T + b + LORA_SCALE * (x @ la.T @ lb.T)
        Bsz, Tlen, Cdim = x.shape
        qkv = lora_linear(x, w_attn, b_attn, la_attn, lb_attn)
        q, k, v = jnp.split(qkv, 3, axis=2)
        rs = lambda t: t.reshape(Bsz, Tlen, H, HD).transpose(0, 2, 1, 3)
        q, k, v = (rs(q), rs(k), rs(v))
        att = jnp.einsum('bhqd,bhkd->bhqk', q, k) * (1.0 / np.sqrt(HD))
        causal = jnp.tril(jnp.ones((Tlen, Tlen), dtype=bool))
        att = jnp.where(causal[None, None], att, -jnp.inf)
        att = jax.nn.softmax(att, axis=-1)
        y = jnp.einsum('bhqk,bhkd->bhqd', att, v)
        y = y.transpose(0, 2, 1, 3).reshape(Bsz, Tlen, Cdim)
        return lora_linear(y, w_proj, b_proj, la_proj, lb_proj)

    def _L0_ffn_ref(x, router_w, gate_proj, up_proj, down_proj):
        import jax, jax.numpy as jnp
        import numpy as np
        NUM_EXPERTS = 8
        TOP_K = 2
        B, T, D, F = (4, 256, 128, 352)
        scores = jnp.einsum('btd,de->bte', x, router_w).astype(jnp.float32)
        probs = jax.nn.softmax(scores, axis=-1)
        routing_weights, routing_idx = jax.lax.top_k(probs, TOP_K)
        routing_weights = (routing_weights / jnp.sum(routing_weights, axis=-1, keepdims=True)).astype(x.dtype)
        one_hot = jax.nn.one_hot(routing_idx, NUM_EXPERTS, dtype=x.dtype)
        expert_w = jnp.einsum('btke,btk->bte', one_hot, routing_weights)
        dispatched = jnp.einsum('btd,btke->bted', x, one_hot)
        gate = jnp.einsum('bted,edf->btef', dispatched, gate_proj)
        up = jnp.einsum('bted,edf->btef', dispatched, up_proj)
        acts = jax.nn.silu(gate) * up
        expert_out = jnp.einsum('btef,efd->bted', acts, down_proj)
        return jnp.einsum('bted,bte->btd', expert_out, expert_w)
    x = L0_attn_x
    x = _layernorm(x + _L0_attn_ref(x, L0_attn_w_attn, L0_attn_b_attn, L0_attn_la_attn, L0_attn_lb_attn, L0_attn_w_proj, L0_attn_b_proj, L0_attn_la_proj, L0_attn_lb_proj), axis=-1)
    x = _layernorm(x + _L0_ffn_ref(x, L0_ffn_router_w, L0_ffn_gate_proj, L0_ffn_up_proj, L0_ffn_down_proj), axis=-1)
    return x

_drawn_inputs = setup_inputs


def setup_inputs(seed=0):
    import zlib

    import numpy as np

    out = dict(_drawn_inputs(seed))
    spreads = {'L0_attn_b_attn': (0.0, 0.398), 'L0_attn_b_proj': (0.0, 0.1)}
    factors = {'L0_attn_w_attn': 8.0,
     'L0_attn_la_attn': 8.0,
     'L0_attn_lb_attn': 8.0,
     'L0_attn_la_proj': 8.0,
     'L0_attn_lb_proj': 8.0,
     'L0_ffn_router_w': 8.0,
     'L0_ffn_gate_proj': 8.0,
     'L0_ffn_up_proj': 8.0,
     'L0_ffn_down_proj': 8.0}
    for name, (base, spread) in spreads.items():
        noise = np.random.default_rng([zlib.crc32(name.encode()), seed]).standard_normal(out[name].shape)
        drawn = base * np.exp(spread * noise) if base else spread * noise
        out[name] = jnp.asarray(drawn.astype(out[name].dtype))
    for name, factor in factors.items():
        out[name] = (out[name] * factor).astype(out[name].dtype)
    return out
```

```python
from contextlib import ExitStack

import concourse.bass as bass
from concourse import mybir

ALU = mybir.AluOpType
ACT = mybir.ActivationFunctionType
F32 = mybir.dt.float32
BF16 = mybir.dt.bfloat16
AX_X = mybir.AxisListType.X

P = 128


def causal_attention_then_top2_experts(
    nc: bass.Bass,
    x: bass.AP, w_attn: bass.AP, b_attn: bass.AP, la_attn: bass.AP, lb_attn: bass.AP,
    w_proj: bass.AP, b_proj: bass.AP, la_proj: bass.AP, lb_proj: bass.AP,
    router_w: bass.AP, gate_proj: bass.AP, up_proj: bass.AP, down_proj: bass.AP,
    out: bass.AP, parts_scratch: bass.AP,
):
    B, T, C = x.shape
    H = 16
    D = C // H
    LORA_R = la_attn.shape[0]
    LORA_SCALE = 0.5
    SCALE = float(D) ** -0.5
    EPS = 1e-5
    NEG = -3.0e38
    E = router_w.shape[1]
    F = gate_proj.shape[2]
    NT = B * T // P
    TB = T // P
    HQ = 4
    QPB = H // HQ
    G = B * QPB
    PARTS = 3
    HALF = P // 2
    FC = [(c, min(P, F - c)) for c in range(0, F, P)]
    NFC = len(FC)
    assert (T, C, D, TB) == (512, P, 8, 4)

    RUNS = [(3, 0), (2, 1), (1, 2)]

    x_tiles = x.rearrange("b (t p) c -> p (b t) c", p=P)
    out_tiles = out.rearrange("b (t p) c -> p (b t) c", p=P)

    with ExitStack() as ctx:
        def sb(name, shape, dt=F32):
            return ctx.enter_context(nc.sbuf_tensor(name, shape, dt))

        def pb(name, shape, dt=F32):
            return ctx.enter_context(nc.psum_tensor(name, shape, dt))

        def sem(name):
            return ctx.enter_context(nc.semaphore(name))

        X = sb("X", [P, NT, C])
        WA = sb("WA", [P, 3, C])
        WP = sb("WP", [P, C])
        LB = sb("LB", [P, 4, LORA_R])
        LA = sb("LA", [LORA_R, 2, C])
        lbT = sb("lbT", [LORA_R, 4, P])
        WT = sb("WT", [P, 3, C])
        WPT = sb("WPT", [P, C])
        bqk = sb("bqk", [P, 2])
        bv_rows = sb("bv_rows", [P, C])
        bp_rows = sb("bp_rows", [P, C])
        identf = sb("identf", [P, P])
        identb = sb("identb", [P, P], BF16)
        maskb = sb("maskb", [P, HQ, P], BF16)
        xT = sb("xT", [P, 2, T])
        qk = sb("qk", [P, 2, T])
        rest = sb("rest", [P, 2, T])
        parts = sb("parts", [P, 2, PARTS, T], BF16)
        Qs = sb("Qs", [P, G, 2, T], BF16)
        Ks = sb("Ks", [P, G, HQ, T], BF16)
        V9 = sb("V9", [P, G, TB, HQ, D + 1])
        vst = sb("vst", [P, 2, TB, HQ, D + 1])
        negm = sb("negm", [P, 2, TB, HQ])
        mrest = sb("mrest", [P, 2, TB, HQ])
        mparts = sb("mparts", [P, 2, TB, HQ, PARTS], BF16)
        mT = sb("mT", [HQ * PARTS, 2, T], BF16)
        PW = [(TB - kb) * P for kb in range(TB)]
        POFF = [HQ * sum(PW[:kb]) for kb in range(TB)]
        Pt = sb("Pt", [P, 2, HQ * sum(PW)])
        pvs = sb("pvs", [P, T])
        rl = sb("rl", [P, TB, HQ])
        Y = sb("Y", [P, B, TB, QPB, HQ, D])
        yT = sb("yT", [P, T])
        stats = sb("stats", [P, TB, 6])
        mv = sb("mv", [P, TB, 2])
        std = sb("std", [P, TB])
        rstd = sb("rstd", [P, TB])
        eps = sb("eps", [P, 1])
        RW = sb("RW", [P, E])
        top = sb("top", [P, NT, 8])
        topi = sb("topi", [P, NT, 8], mybir.dt.uint32)
        topf = sb("topf", [P, NT, 2])
        lanes = sb("lanes", [P, NT, E])
        hot = sb("hot", [P, 2, NT, E])
        sc = sb("sc", [P, NT, E])
        ex = sb("ex", [P, NT, E])
        wsum = sb("wsum", [P, NT])
        wts = sb("wts", [P, NT, E])
        free = Ks[:, :, :, :].rearrange("p g h t -> p (g h t)").bitcast(F32)
        GW = free[:, 0:E * F].rearrange("p (e f) -> p e f", e=E)
        UW = free[:, E * F:2 * E * F].rearrange("p (e f) -> p e f", e=E)
        DW = free[:, 2 * E * F:2 * E * F + E * NFC * C].rearrange("p (e k c) -> p e k c", e=E, k=NFC)
        free_q = Qs[:, :, :, :].rearrange("p g h t -> p (g h t)").bitcast(F32)
        x1T = free_q[:, 0:B * T]
        sg = free_q[:, B * T:B * T + 3 * T].rearrange("p (n t) -> p n t", n=3)
        hT = Pt[:, 0, 0:2 * NFC * T // 1].rearrange("p (n k t) -> p n k t", n=2, k=NFC) if 2 * NFC * T <= HQ * sum(PW) else None

        slot = [pb(f"slot{i}", [P, 2 * T]) for i in range(3)]
        pvo = pb("pvo", [P, T])
        misc = pb("misc", [P, T])
        miscb = misc[:, :].bitcast(BF16)

        w_loaded = sem("w_loaded")
        x_loaded = [sem(f"x_loaded{b}") for b in range(B)]
        consts_ready = sem("consts_ready")
        ident0 = sem("ident0")
        stacks_zeroed = sem("stacks_zeroed")
        kones_zeroed = sem("kones_zeroed")
        qzeroed = sem("qzeroed")
        weights_full = sem("weights_full")
        weights_out = sem("weights_out")
        xT_full, xT_out = sem("xT_full"), sem("xT_out")
        q_full, k_full, v_full = sem("q_full"), sem("k_full"), sem("v_full")
        q_out, k_out, v_out = sem("q_out"), sem("k_out"), sem("v_out")
        qsplit, ksplit = sem("qsplit"), sem("ksplit")
        qchain, kchain = sem("qchain"), sem("kchain")
        parts_stored = [[sem(f"parts_stored{s}{b}") for b in range(B)] for s in range(2)]
        stacks_loaded = [sem(f"stacks_loaded{b}") for b in range(B)]
        scores_for_max, max_done = sem("scores_for_max"), sem("max_done")
        scores_for_exp, exp_done = sem("scores_for_exp"), sem("exp_done")
        mchain, mparts_ready = sem("mchain"), sem("mparts_ready")
        mT_full, mT_copied = sem("mT_full"), sem("mT_copied")
        maxrows = [sem("maxrows0"), sem("maxrows1")]
        selected, vst_ready = sem("selected"), sem("vst_ready")
        pv_done, pvs_copied = sem("pv_done"), sem("pvs_copied")
        yT_full, rl_ready, y_done = sem("yT_full"), sem("rl_ready"), sem("y_done")
        ychain = sem("ychain")
        out_stored = sem("out_stored")
        pool_passed = sem("pool_passed")
        xb_ready = sem("xb_ready")
        experts_loaded = sem("experts_loaded")
        fT_full, fT_out, proj_full, stats_ready, std_ready = (sem(n) for n in ("fT_full", "fT_out", "proj_full", "stats_ready", "std_ready"))
        lchain, x1_ready, x1T_full, x1T_out = (sem(n) for n in ("lchain", "x1_ready", "x1T_full", "x1T_out"))
        router_full, lanes_ready, sub_ready, ex_ready, wts_ready = (sem(n) for n in ("router_full", "lanes_ready", "sub_ready", "ex_ready", "wts_ready"))
        gate_full, up_full, silu_done, h_ready, down_full, acc_done = (sem(n) for n in ("gate_full", "up_full", "silu_done", "h_ready", "down_full", "acc_done"))
        stats2, std2, norm2 = (sem(n) for n in ("stats2", "std2", "norm2"))

        S_UNITS = [(3, 0, 2), (3, 2, 2), (2, 0, 2), (2, 2, 2), (1, 0, 4), (0, 0, 4)]
        T_UNITS = [(0, 0, 2), (0, 2, 2), (1, 0, 2), (1, 2, 2), (2, 0, 4), (3, 0, 4)]
        NU = len(S_UNITS)
        W_DMAS = 11

        def s_view(u, n):
            qb, _, heads = S_UNITS[u]
            return slot[n][:, :].rearrange("p (h k) -> p h k", k=[128, 256, 512, 512][qb])[:, 0:heads, 0:(qb + 1) * P]

        def t_view(u, n):
            kb, _, heads = T_UNITS[u]
            return slot[n][:, :].rearrange("p (h k) -> p h k", k=[512, 512, 256, 128][kb])[:, 0:heads, 0:PW[kb]]

        def p_view(par, kb):
            return Pt[:, par, POFF[kb]:POFF[kb] + HQ * PW[kb]].rearrange("p (h q) -> p h q", h=HQ)

        block = ctx.enter_context(nc.Block())

        @block.sync
        def _(sp):
            for b in range(B):
                sp.dma_start(X[:, b * TB:(b + 1) * TB, :], x_tiles[:, b * TB:(b + 1) * TB, :]).then_inc(x_loaded[b], 16)
                if b == 0:
                    sp.dma_start(WA[:, :, :], w_attn.rearrange("(j p) c -> p j c", p=P)).then_inc(w_loaded, 16)
                    sp.dma_start(LB[:, 0:3, :], lb_attn.rearrange("(j p) r -> p j r", p=P)).then_inc(w_loaded, 16)
                    sp.dma_start(LB[:, 3, :], lb_proj).then_inc(w_loaded, 16)
                    sp.dma_start(LA[:, 0, :], la_attn).then_inc(w_loaded, 16)
                    sp.dma_start(LA[:, 1, :], la_proj).then_inc(w_loaded, 16)
                    sp.dma_start(WP[:, :], w_proj).then_inc(w_loaded, 16)
                    sp.dma_start(RW[:, :], router_w).then_inc(w_loaded, 16)
                    for j in range(2):
                        sp.dma_start(bqk[:, j:j + 1], b_attn[j * C:(j + 1) * C].rearrange("(p a) -> p a", a=1)).then_inc(w_loaded, 16)
                    sp.dma_start(bv_rows[:, :], b_attn[2 * C:3 * C].rearrange("(a c) -> a c", a=1).broadcast_to([P, C])).then_inc(w_loaded, 16)
                    sp.dma_start(bp_rows[:, :], b_proj.rearrange("(a c) -> a c", a=1).broadcast_to([P, C])).then_inc(w_loaded, 16)
            sp.wait_ge(stacks_zeroed, 1)
            sp.wait_ge(kones_zeroed, 3)
            for b in range(B):
                for s, split in ((0, qsplit), (1, ksplit)):
                    sp.wait_ge(split, b + 1)
                    sp.dma_start(parts_scratch[b, s].rearrange("e p t -> p e t"), parts[:, s]).then_inc(parts_stored[s][b], 16)
                for s in range(2):
                    sp.wait_ge(parts_stored[s][b], 16)
                    src = parts_scratch[b, s].rearrange("e (j a d) t -> a e d j t", a=2, d=D)
                    for a in range(2):
                        row = HALF * a + PARTS
                        for n, kpart in RUNS:
                            for e in range(n):
                                if s == 0:
                                    dst = Qs[row:row + D, QPB * b:QPB * (b + 1)].rearrange("p g c t -> p (g c) t")
                                else:
                                    dst = Ks[row:row + D, QPB * b:QPB * (b + 1)].rearrange("p g (c a) t -> p a (g c) t", a=2)[:, a]
                                sp.dma_start(dst, src[a, e if s == 0 else kpart]).then_inc(stacks_loaded[b], 16)
                                row += D

            def store_maxrows(g, par):
                sp.wait_ge(mT_copied, g + 1)
                for h in range(HQ):
                    sp.dma_start(Qs[HALF * (h % 2):HALF * (h % 2) + PARTS, bass.ds(g, 1), h // 2, :],
                                 mT[PARTS * h:PARTS * (h + 1), par, :]).then_inc(maxrows[par], 16)

            store_maxrows(0, 0)
            store_maxrows(1, 1)
            with sp.Fori(1, G // 2 - 1) as pair:
                g = 2 * pair
                store_maxrows(g, 0)
                store_maxrows(g + 1, 1)
            store_maxrows(14, 0)
            store_maxrows(15, 1)
            sp.wait_ge(scores_for_exp, NU * G)
            for w, dst in ((gate_proj, GW), (up_proj, UW)):
                sp.dma_start(dst, w.rearrange("e d f -> d e f")).then_inc(experts_loaded, 16)
            for k, (f0, fn) in enumerate(FC):
                sp.dma_start(DW[0:fn, :, k, :], down_proj[:, f0:f0 + fn, :].rearrange("e f c -> f e c")).then_inc(experts_loaded, 16)
            for b in range(B):
                sp.wait_ge(norm2, b + 1)
                sp.dma_start(out_tiles[:, b * TB:(b + 1) * TB, :], X[:, b * TB:(b + 1) * TB, :]).then_inc(out_stored, 16)
            sp.wait_ge(out_stored, 16 * B)

        STACK_DMAS = 2 * 2 * 6 * 16

        @block.gpsimd
        def _(pool):
            pool.memset(identf[:, :], 0.0).then_inc(ident0, 1)
            pool.memset(maskb[:, :, :], 0.0).then_inc(ident0, 1)
            pool.wait_ge(ident0, 2)
            pool.affine_select(out=identf[:, :], in_=identf[:, :], compare_op=ALU.not_equal, fill=1.0,
                               base=0, pattern=[[-1, P]], channel_multiplier=1).then_inc(consts_ready, 1)
            pool.affine_select(out=maskb[:, :, :], in_=maskb[:, :, :], compare_op=ALU.is_ge, fill=NEG,
                               base=0, pattern=[[0, HQ], [-1, P]], channel_multiplier=1).then_inc(consts_ready, 1)
            pool.wait_ge(consts_ready, 2)
            pool.tensor_copy(identb[:, :], identf[:, :]).then_inc(consts_ready, 1)
            pool.memset(Ks[:, :, :, :].rearrange("p g h t -> p (g h t)").bitcast(F32), 0.0).then_inc(kones_zeroed, 1)
            pool.wait_ge(kones_zeroed, 1)
            for a in range(2):
                pool.memset(Ks[HALF * a:HALF * a + PARTS, :, a:HQ:2, :], 1.0).then_inc(kones_zeroed, 1)
            pool.wait_ge(kones_zeroed, 3)
            n = 0
            for b in range(B):
                pool.wait_ge(k_out, b + 1)
                if b:
                    pool.wait_ge(parts_stored[1][b - 1], 16)
                for e in range(PARTS - 1):
                    pool.tensor_copy(parts[:, 1, e, :], qk[:, 1, :] if e == 0 else rest[:, 1, :]).then_inc(kchain, 1)
                    n += 1
                    pool.wait_ge(kchain, n)
                    last = pool.tensor_tensor(rest[:, 1, :] if e == 0 else parts[:, 1, 2, :],
                                              qk[:, 1, :] if e == 0 else rest[:, 1, :], parts[:, 1, e, :], ALU.subtract)
                    if e == 0:
                        last.then_inc(kchain, 1)
                        n += 1
                        pool.wait_ge(kchain, n)
                last.then_inc(ksplit, 1)

            pool.memset(eps[:, :], EPS)
            pool.iota(lanes[:, :, :], pattern=[[0, NT], [1, E]], base=0, channel_multiplier=0,
                      allow_small_or_imprecise_dtypes=True).then_inc(lanes_ready, 1)
            pool.wait_ge(xT_full, B)
            for t in range(NT):
                last = pool.tensor_tensor(X[:, t, :], X[:, t, :], bp_rows[:, :], ALU.add)
            last.then_inc(xb_ready, 1)

            def wait_counted(semaphore, count):
                pool.wait_ge(semaphore, count)
                pool.sem_inc(pool_passed, 1)

            def split_max(g, par):
                wait_counted(max_done, NU * g + NU)
                if not isinstance(g, int) or g >= 2:
                    wait_counted(mT_full, g - 1)
                m = negm[:, par]
                r = mrest[:, par]
                p = [mparts[:, par, :, :, e] for e in range(PARTS)]
                pool.tensor_copy(p[0], m).then_inc(mchain, 1)
                pool.wait_ge(mchain, 3 * g + 1)
                pool.tensor_tensor(r, m, p[0], ALU.subtract).then_inc(mchain, 1)
                wait_counted(mchain, 3 * g + 2)
                pool.tensor_copy(p[1], r).then_inc(mchain, 1)
                pool.wait_ge(mchain, 3 * g + 3)
                pool.tensor_tensor(p[2], r, p[1], ALU.subtract).then_inc(mparts_ready, 1)

            def select(g, par, kb):
                wait_counted(exp_done, NU * g + [2, 4, 5, 6][kb])
                v = p_view(par, kb)[:, :, 0:P]
                pool.affine_select(out=v, in_=v, compare_op=ALU.is_ge, fill=0.0, base=0,
                                   pattern=[[0, HQ], [1, P]], channel_multiplier=-1).then_inc(selected, 1)

            def step(g, par, first=False, scores=True):
                if not first:
                    wait_counted(pv_done, g - 1)
                pool.tensor_copy(vst[:, par].rearrange("p t h d -> p (t h d)"),
                                 V9[:, bass.ds(g, 1)].rearrange("p g t h d -> p (g t h d)")).then_inc(vst_ready, 1)
                for kb in range(TB):
                    select(g, par, kb)
                if scores:
                    split_max(g + 2, par)

            split_max(0, 0)
            split_max(1, 1)
            pool.wait_ge(v_out, B)
            step(0, 0, first=True)
            step(1, 1, first=True)
            with pool.Fori(1, G // 2 - 1) as pair:
                g = 2 * pair
                step(g, 0)
                step(g + 1, 1)
            step(14, 0, scores=False)
            step(15, 1, scores=False)

        @block.scalar
        def _(act):
            for b in range(B):
                act.wait_ge(xT_full, b + 1)
                if b >= 2:
                    act.wait_ge(v_full, b - 1)
                act.activation(xT[:, b % 2, :], misc[:, :], ACT.Copy).then_inc(xT_out, 1)
                act.wait_ge(q_full, b + 1)
                if b == 0:
                    act.wait_ge(w_loaded, 16 * W_DMAS)
                else:
                    act.wait_ge(qsplit, b)
                act.activation(qk[:, 0, :], slot[0][:, 0:T], ACT.Identity, bias=bqk[:, 0:1]).then_inc(q_out, 1)
                act.wait_ge(k_full, b + 1)
                if b:
                    act.wait_ge(ksplit, b)
                act.activation(qk[:, 1, :], slot[0][:, T:2 * T], ACT.Identity, bias=bqk[:, 1:2]).then_inc(k_out, 1)

            def copy_mT(g, par):
                act.wait_ge(mT_full, g + 1)
                act.activation(mT[:, par, :], miscb[0:HQ * PARTS, 0:T], ACT.Copy).then_inc(mT_copied, 1)

            def copy_pv(g, first=False):
                act.wait_ge(pv_done, g + 1)
                if not first:
                    act.wait_ge(yT_full, g)
                act.activation(pvs[:, :], pvo[:, :], ACT.Copy).then_inc(pvs_copied, 1)

            def step(g, par, exps=True, pv=True, maxrows=True, first_pv=False):
                for u in range(NU):
                    if exps:
                        kb, h0, heads = T_UNITS[u]
                        act.wait_ge(scores_for_exp, NU * g + u + 1)
                        if u == 0 and pv and not first_pv:
                            act.wait_ge(pv_done, g - 1)
                        act.activation(p_view(par, kb)[:, h0:h0 + heads, :], t_view(u, (2 * u + 1) % 3), ACT.Exp,
                                       scale=SCALE).then_inc(exp_done, 1)
                    if u == 2 and pv:
                        copy_pv(g - 1, first=first_pv)
                    if u == 3 and maxrows:
                        copy_mT(g + 1, 1 - par)

            copy_mT(0, 0)
            step(0, 0, pv=False)
            step(1, 1, first_pv=True)
            with act.Fori(1, G // 2 - 1) as pair:
                g = 2 * pair
                step(g, 0)
                step(g + 1, 1)
            step(14, 0)
            step(15, 1, maxrows=False)
            step(16, 0, exps=False, maxrows=False)
            for b in range(B):
                act.wait_ge(fT_full, b + 1)
                if b:
                    act.wait_ge(proj_full, b)
                act.activation(yT[:, :], slot[0][:, 0:T], ACT.Copy).then_inc(fT_out, 1)
                act.wait_ge(stats_ready, b + 1)
                act.activation(std[:, :], mv[:, :, 1], ACT.Sqrt, bias=eps[:, 0:1]).then_inc(std_ready, 1)
                act.wait_ge(x1T_full, b + 1)
                act.activation(x1T[:, b * T:(b + 1) * T], slot[2][:, 0:T], ACT.Copy).then_inc(x1T_out, 1)
            act.wait_ge(sub_ready, 1)
            act.activation(ex[:, :, :], sc[:, :, :], ACT.Exp).then_inc(ex_ready, 1)
            with act.Fori(0, B) as t:
                for e in range(E):
                    for k, (f0, fn) in enumerate(FC):
                        act.wait_ge(gate_full, NFC * (E * t + e) + k + 1)
                        act.wait_ge(h_ready, NFC * (E * t + e) + k + 1)
                        act.activation(sg[0:fn, k, :], slot[k][0:fn, 0:T], ACT.Silu).then_inc(silu_done, 1)
            for b in range(B):
                act.wait_ge(stats2, b + 1)
                act.activation(std[:, :], mv[:, :, 1], ACT.Sqrt, bias=eps[:, 0:1]).then_inc(std2, 1)

        @block.vector
        def _(dve):
            dve.memset(Qs[:, :, :, :].rearrange("p g h t -> p (g h t)").bitcast(F32), 0.0).then_inc(stacks_zeroed, 1)
            dve.memset(pvo[:, :], 0.0).then_inc(qzeroed, 1)
            dve.memset(V9[:, :, :, :, D:D + 1], 1.0)
            dve.wait_ge(weights_full, 1)
            dve.tensor_scalar(lbT[:, :, :].rearrange("r j p -> r (j p)"), slot[1][0:LORA_R, 0:T], LORA_SCALE, None,
                              ALU.mult).then_inc(weights_out, 1)
            dve.wait_ge(weights_full, 2)
            dve.tensor_copy(WT[:, :, :].rearrange("p j c -> p (j c)"), slot[2][:, 0:3 * C]).then_inc(weights_out, 1)
            dve.tensor_copy(WPT[:, :], slot[2][:, T:T + C]).then_inc(weights_out, 1)
            n = 0
            for b in range(B):
                dve.wait_ge(q_out, b + 1)
                if b:
                    dve.wait_ge(parts_stored[0][b - 1], 16)
                for e in range(PARTS - 1):
                    dve.tensor_copy(parts[:, 0, e, :], qk[:, 0, :] if e == 0 else rest[:, 0, :]).then_inc(qchain, 1)
                    n += 1
                    dve.wait_ge(qchain, n)
                    last = dve.tensor_tensor(rest[:, 0, :] if e == 0 else parts[:, 0, 2, :],
                                             qk[:, 0, :] if e == 0 else rest[:, 0, :], parts[:, 0, e, :], ALU.subtract)
                    if e == 0:
                        last.then_inc(qchain, 1)
                        n += 1
                        dve.wait_ge(qchain, n)
                last.then_inc(qsplit, 1)
                dve.wait_ge(v_full, b + 1)
                if b == 0:
                    dve.wait_ge(w_loaded, 16 * W_DMAS)
                for t in range(TB):
                    last = dve.tensor_tensor(V9[:, QPB * b:QPB * (b + 1), t, :, 0:D],
                                             slot[1][:, T + t * C:T + (t + 1) * C].rearrange("p (i h d) -> p i h d", i=QPB, h=HQ),
                                             bv_rows[:, :].rearrange("p (i h d) -> p i h d", i=QPB, h=HQ), ALU.add)
                last.then_inc(v_out, 1)

            def row_max(g, par, u, n, first=False):
                qb, h0, heads = S_UNITS[u]
                dve.wait_ge(scores_for_max, NU * g + u + 1)
                if u == 0 and not first:
                    dve.wait_ge(mparts_ready, g - 1)
                dve.tensor_reduce(negm[:, par, qb, h0:h0 + heads], s_view(u, n), AX_X, ALU.max,
                                  negate=True).then_inc(max_done, 1)

            def normalize(g):
                dve.wait_ge(yT_full, g + 1)
                v = misc[:, :].rearrange("p (t h e) -> p t h e", t=TB, h=HQ)
                dve.reciprocal(rl[:, :, :], v[:, :, :, D]).then_inc(rl_ready, 1)
                dve.wait_ge(rl_ready, g + 1)
                dve.tensor_tensor(Y[:, bass.ds(g // QPB, 1), :, bass.ds(g % QPB, 1)].rearrange("p b t i h d -> p (b t i) h d"), v[:, :, :, 0:D],
                                  rl[:, :, :].rearrange("p t (h a) -> p t h a", a=1).broadcast_to([P, TB, HQ, D]), ALU.mult).then_inc(y_done, 1)

            def step(g, par, scores=True, pv=True):
                for u in range(NU):
                    if scores:
                        row_max(g + 2, par, u, (2 * u) % 3)
                    if u == 4 and pv:
                        normalize(g - 1)

            for g in range(2):
                for u in range(NU):
                    row_max(g, g, u, (NU * g + u) % 3, first=True)
            step(0, 0, pv=False)
            step(1, 1)
            with dve.Fori(1, G // 2 - 1) as pair:
                g = 2 * pair
                step(g, 0)
                step(g + 1, 1)
            step(14, 0, scores=False)
            step(15, 1, scores=False)
            step(16, 0, scores=False)

            class Chain:
                count = 0

            def link(instruction):
                Chain.count += 1
                instruction.then_inc(lchain, 1)
                dve.wait_ge(lchain, Chain.count)

            def statistics(b, done):
                for t in range(TB):
                    last = dve.bn_stats(stats[:, t, :], X[:, b * TB + t, :])
                link(last)
                for t in range(TB):
                    last = dve.bn_aggr(mv[:, t, :], stats[:, t, :])
                last.then_inc(done, 1)

            def normed(b, std_done, done):
                dve.wait_ge(std_done, b + 1)
                link(dve.reciprocal(rstd[:, :], std[:, :]))
                for t in range(TB):
                    last = dve.tensor_scalar(X[:, b * TB + t, :], X[:, b * TB + t, :], mv[:, t, 0:1], rstd[:, t:t + 1],
                                             ALU.subtract, ALU.mult)
                last.then_inc(done, 1)

            dve.wait_ge(xb_ready, 1)
            for b in range(B):
                dve.wait_ge(proj_full, b + 1)
                xb = X[:, b * TB:(b + 1) * TB, :].rearrange("p t c -> p (t c)")
                link(dve.tensor_tensor(xb, slot[1][:, 0:T], xb, ALU.add))
                statistics(b, stats_ready)
                normed(b, std_ready, x1_ready)
            dve.wait_ge(router_full, 1)
            dve.wait_ge(lanes_ready, 1)
            scores = pvo[:, 0:NT * E].rearrange("p (t e) -> p t e", e=E)
            link(dve.tensor_copy(sc[:, :, :], scores))
            for t in range(NT):
                last = dve.max(top[:, t, :], sc[:, t, :])
            link(last)
            for t in range(NT):
                last = dve.max_index(topi[:, t, :], top[:, t, :], sc[:, t, :])
            link(last)
            link(dve.tensor_copy(topf[:, :, :], topi[:, :, 0:2]))
            for j in range(2):
                last = dve.tensor_tensor(hot[:, j], lanes[:, :, :], topf[:, :, j:j + 1].broadcast_to([P, NT, E]), ALU.is_equal)
            link(last)
            link(dve.tensor_tensor(hot[:, 0], hot[:, 0], hot[:, 1], ALU.add))
            dve.tensor_tensor(sc[:, :, :], sc[:, :, :], top[:, :, 0:1].broadcast_to([P, NT, E]), ALU.subtract).then_inc(sub_ready, 1)
            dve.wait_ge(ex_ready, 1)
            link(dve.tensor_tensor(ex[:, :, :], ex[:, :, :], hot[:, 0], ALU.mult))
            link(dve.tensor_reduce(wsum[:, :], ex[:, :, :], AX_X, ALU.add))
            link(dve.reciprocal(wsum[:, :], wsum[:, :]))
            dve.tensor_tensor(wts[:, :, :], ex[:, :, :], wsum[:, :].rearrange("p (t a) -> p t a", a=1).broadcast_to([P, NT, E]),
                              ALU.mult).then_inc(wts_ready, 1)
            dve.wait_ge(wts_ready, 1)

            def hidden(t, e):
                n = E * t + e
                for k, (f0, fn) in enumerate(FC):
                    dve.wait_ge(silu_done, NFC * n + k + 1)
                    dve.wait_ge(up_full, NFC * n + k + 1)
                    dve.tensor_tensor(hT[0:fn, e % 2, k, :], slot[k][0:fn, T:2 * T], sg[0:fn, k, :], ALU.mult).then_inc(h_ready, 1)

            def accumulate(t, e, prev):
                n = E * t + e
                dve.wait_ge(down_full, n + 1)
                bank = (misc, pvo)[e % 2]
                for q in range(TB):
                    tile = t * TB + q
                    acc = X[:, bass.ds(tile, 1), :].rearrange("p t c -> p (t c)")
                    last = dve.scalar_tensor_tensor(out=acc, in0=bank[:, q * C:(q + 1) * C],
                                                    scalar=wts[:, bass.ds(tile, 1), e:e + 1].rearrange("p t c -> p (t c)"), in1=acc, op0=ALU.mult, op1=ALU.add)
                last.then_inc(acc_done, 1)

            dve.tensor_copy(hot[:, 1], hot[:, 0]).then_inc(h_ready, NFC)
            dve.tensor_copy(topf[:, :, :], topi[:, :, 0:2]).then_inc(acc_done, 2)
            with dve.Fori(0, B) as t:
                for e in range(E):
                    hidden(t, e)
                    if e:
                        dve.wait_ge(acc_done, E * t + e + 1)
                        accumulate(t, e - 1, None)
                dve.wait_ge(acc_done, E * t + E + 1)
                accumulate(t, E - 1, None)
            dve.wait_ge(acc_done, E * B + 2)
            for b in range(B):
                statistics(b, stats2)
                normed(b, std2, norm2)

        @block.tensor
        def _(pe):
            def transpose_x(b):
                pe.wait_ge(x_loaded[b], 16)
                if b:
                    pe.wait_ge(xT_out, b)
                for t in range(TB):
                    last = pe.transpose(misc[:, t * P:(t + 1) * P], X[:, b * TB + t, :], identf[:, :])
                last.then_inc(xT_full, 1)

            pe.wait_ge(consts_ready, 3)
            transpose_x(0)
            pe.wait_ge(w_loaded, 16 * W_DMAS)
            for j in range(4):
                last = pe.transpose(slot[1][0:LORA_R, j * P:(j + 1) * P], LB[:, j, :], identf[:, :])
            last.then_inc(weights_full, 1)
            pe.wait_ge(weights_out, 1)
            for j in range(3):
                pe.matmul(slot[2][:, j * C:(j + 1) * C], WA[:, j, :], identf[:, :], start=(j == 0), stop=False, skip_group_check=True)
            pe.matmul(slot[2][:, 0:3 * C], LA[:, 0, :], lbT[:, 0:3, :].rearrange("r j p -> r (j p)"), start=False, stop=True, skip_group_check=True)
            pe.matmul(slot[2][:, T:T + C], WP[:, :], identf[:, :], start=True, stop=False, skip_group_check=True)
            pe.matmul(slot[2][:, T:T + C], LA[:, 1, :], lbT[:, 3, :], start=False, stop=True, skip_group_check=True).then_inc(weights_full, 1)
            for b in range(B):
                pe.wait_ge(xT_out, b + 1)
                if b == 0:
                    pe.wait_ge(weights_out, 3)
                for j, full, done in ((0, q_full, q_out), (1, k_full, k_out)):
                    if b:
                        pe.wait_ge(done, b)
                    pe.matmul(slot[0][:, j * T:(j + 1) * T], WT[:, j, :], xT[:, b % 2, :], start=True, stop=True).then_inc(full, 1)
                if b + 1 < B:
                    transpose_x(b + 1)
                if b:
                    pe.wait_ge(v_out, b)
                for t in range(TB):
                    last = pe.matmul(slot[1][:, T + t * C:T + (t + 1) * C], xT[:, b % 2, t * P:(t + 1) * P], WT[:, 2, :], start=True, stop=True)
                last.then_inc(v_full, 1)

            def scores_q(g, u, n):
                qb, h0, heads = S_UNITS[u]
                v = s_view(u, n)
                per_bank = {3: 1, 2: 1, 1: 2, 0: 4}[qb]
                for h in range(0, heads, per_bank):
                    pe.matmul(v[:, h:h + per_bank, qb * P:(qb + 1) * P], identb[:, :], maskb[:, 0:per_bank, :],
                              start=True, stop=False, skip_group_check=True)
                    for j in range(h, h + per_bank):
                        head = h0 + j
                        last = pe.matmul(v[:, j, :], Qs[:, bass.ds(g, 1), head // 2, qb * P:(qb + 1) * P],
                                         Ks[:, bass.ds(g, 1), head, 0:(qb + 1) * P],
                                         start=False, stop=True, skip_group_check=True)
                last.then_inc(scores_for_max, 1)

            def scores_k(g, u, n):
                kb, h0, heads = T_UNITS[u]
                v = t_view(u, n)
                for j in range(heads):
                    head = h0 + j
                    last = pe.matmul(v[:, j, :], Ks[:, bass.ds(g, 1), head, kb * P:(kb + 1) * P],
                                     Qs[:, bass.ds(g, 1), head // 2, kb * P:T], start=True, stop=True)
                last.then_inc(scores_for_exp, 1)

            def transpose_max(g, par, drained=None):
                pe.wait_ge(mparts_ready, g + 1)
                if drained is not None:
                    pe.wait_ge(y_done, drained)
                for t in range(TB):
                    last = pe.transpose(miscb[0:HQ * PARTS, t * P:(t + 1) * P],
                                        mparts[:, par, t].rearrange("p h e -> p (h e)"), identb[:, :])
                last.then_inc(mT_full, 1)

            def weighted_values(g, par, kb):
                pe.wait_ge(selected, TB * g + kb + 1)
                if kb == 0:
                    pe.wait_ge(vst_ready, g + 1)
                    pe.wait_ge(pvs_copied, g)
                for h in range(HQ):
                    last = pe.matmul(pvo[32 * h:32 * h + D + 1, kb * P:T], vst[:, par, kb, h, :], p_view(par, kb)[:, h, :],
                                     start=(kb == 0), stop=(kb == TB - 1))
                if kb == TB - 1:
                    last.then_inc(pv_done, 1)

            def transpose_pv(g):
                pe.wait_ge(pvs_copied, g + 1)
                pe.wait_ge(mT_copied, min(g + 3, G) if isinstance(g, int) else g + 3)
                if not (isinstance(g, int) and g == 0):
                    pe.wait_ge(y_done, g)
                for t in range(TB):
                    last = pe.transpose(misc[:, t * P:(t + 1) * P], pvs[:, t * P:(t + 1) * P], identf[:, :])
                last.then_inc(yT_full, 1)

            def step(g, par, first=False, scores=True, exps=True, maxrows=True):
                for u in range(NU):
                    if scores:
                        if first:
                            pe.wait_ge(max_done, NU * 2)
                        if not first or u >= 2:
                            pe.wait_ge(exp_done, NU * g + u - 1)
                        scores_q(g + 2, u, (2 * u) % 3)
                    if exps:
                        if u == 0:
                            pe.wait_ge(maxrows_sem(par), 32 * (g - par) + 64)
                        if scores:
                            pe.wait_ge(max_done, NU * g + 2 * NU + u)
                        else:
                            pe.wait_ge(max_done, NU * G)
                            pe.wait_ge(exp_done, NU * g + u - 2)
                        scores_k(g, u, (2 * u + 1) % 3)
                    if not first:
                        if u < 2:
                            weighted_values(g - 1, 1 - par, u)
                        if u == 2:
                            weighted_values(g - 1, 1 - par, 2)
                            weighted_values(g - 1, 1 - par, 3)
                    if u == 3 and maxrows:
                        transpose_max(g + 1, 1 - par, drained=None if first else g - 1)
                    if u == 4 and not first:
                        transpose_pv(g - 1)

            def maxrows_sem(par):
                return maxrows[par]

            pe.wait_ge(qzeroed, 1)
            pe.wait_ge(stacks_loaded[0], STACK_DMAS)
            pe.wait_ge(k_out, B)
            pe.wait_ge(v_out, B)
            for g in range(2):
                for u in range(NU):
                    n = NU * g + u
                    if n >= 3:
                        pe.wait_ge(max_done, n - 2)
                    scores_q(g, u, n % 3)
                if g == 0:
                    pe.wait_ge(xT_out, B)
                    transpose_max(0, 0)
            step(0, 0, first=True)
            for b in range(1, B):
                pe.wait_ge(stacks_loaded[b], STACK_DMAS)
            step(1, 1)
            with pe.Fori(1, G // 2 - 1) as pair:
                g = 2 * pair
                step(g, 0)
                step(g + 1, 1)
            step(14, 0, scores=False)
            step(15, 1, scores=False, maxrows=False)
            step(16, 0, scores=False, exps=False, maxrows=False)
            pe.wait_ge(y_done, G)
            pe.wait_ge(exp_done, NU * G)

            def norm_tail(b):
                pe.wait_ge(x1_ready, b + 1)
                if b:
                    pe.wait_ge(x1T_out, b)
                for t in range(TB):
                    last = pe.transpose(slot[2][:, t * P:(t + 1) * P], X[:, b * TB + t, :], identf[:, :])
                last.then_inc(x1T_full, 1)
                pe.wait_ge(x1T_out, b + 1)
                for t in range(b * TB, (b + 1) * TB):
                    last = pe.matmul(pvo[:, t * E:(t + 1) * E], x1T[:, t * P:(t + 1) * P], RW[:, :], start=True, stop=True)
                if b == B - 1:
                    last.then_inc(router_full, 1)

            for b in range(B):
                if b:
                    pe.wait_ge(fT_out, b)
                for t in range(TB):
                    last = pe.transpose(slot[0][:, t * P:(t + 1) * P], Y[:, b, t].rearrange("p i h d -> p (i h d)"), identf[:, :])
                last.then_inc(fT_full, 1)
                pe.wait_ge(fT_out, b + 1)
                if b:
                    pe.wait_ge(stats_ready, b)
                for t in range(TB):
                    last = pe.matmul(slot[1][:, t * C:(t + 1) * C], yT[:, t * P:(t + 1) * P], WPT[:, :], start=True, stop=True)
                last.then_inc(proj_full, 1)
                norm_tail(b)
            pe.wait_ge(wts_ready, 1)
            pe.wait_ge(experts_loaded, 16 * (2 + NFC))

            def gate_up(t, e):
                for k, (f0, fn) in enumerate(FC):
                    pe.wait_ge(h_ready, NFC * (E * t + e) + k + 1)
                    pe.matmul(slot[k][0:fn, 0:T], GW[:, e, f0:f0 + fn], x1T[:, bass.ds(t * T, T)], start=True, stop=True).then_inc(gate_full, 1)
                    pe.matmul(slot[k][0:fn, T:2 * T], UW[:, e, f0:f0 + fn], x1T[:, bass.ds(t * T, T)], start=True, stop=True).then_inc(up_full, 1)

            def down(t, e):
                pe.wait_ge(h_ready, NFC * (E * t + e) + 2 * NFC)
                bank = (misc, pvo)[e % 2]
                pe.wait_ge(acc_done, E * t + e + 1)
                for q in range(TB):
                    for k, (f0, fn) in enumerate(FC):
                        last = pe.matmul(bank[:, q * C:(q + 1) * C], hT[0:fn, e % 2, k, q * P:(q + 1) * P], DW[0:fn, e, k, :],
                                         start=(k == 0), stop=(k == NFC - 1))
                last.then_inc(down_full, 1)

            with pe.Fori(0, B) as t:
                for e in range(E):
                    gate_up(t, e)
                    if e:
                        down(t, e - 1)
                down(t, E - 1)


_INS = ['L0_attn_x', 'L0_attn_w_attn', 'L0_attn_b_attn', 'L0_attn_la_attn', 'L0_attn_lb_attn', 'L0_attn_w_proj',
        'L0_attn_b_proj', 'L0_attn_la_proj', 'L0_attn_lb_proj', 'L0_ffn_router_w', 'L0_ffn_gate_proj',
        'L0_ffn_up_proj', 'L0_ffn_down_proj']
_OUTS = [((4, 512, 128), 'float32')]


def kernel(**inputs):
    import numpy as _np
    import concourse.bacc as _bacc
    from concourse import mybir as _mybir
    from concourse.bass_utils import run_bass_kernel_spmd as _run

    nc = _bacc.Bacc("TRN2", target_bir_lowering=False, num_devices=1)
    arrays, args = {}, []
    for name in _INS:
        a = _np.ascontiguousarray(inputs[name])
        arrays[f"in_{name}_dram"] = a
        args.append(nc.dram_tensor(f"in_{name}_dram", a.shape, _mybir.dt.from_np(a.dtype), kind="ExternalInput").ap())
    for i, (shape, dtype) in enumerate(_OUTS):
        dt = _mybir.dt.from_np(_np.dtype(dtype))
        args.append(nc.dram_tensor(f"out_{i}_dram", shape, dt, kind="ExternalOutput").ap())
    args.append(nc.dram_tensor("parts_scratch", (4, 2, 3, 128, 512), _mybir.dt.bfloat16).ap())
    causal_attention_then_top2_experts(nc, *args)
    r = _run(nc, [arrays], core_ids=[0])
    return r.results[0]["out_0_dram"]
```

```python
from contextlib import ExitStack

import concourse.bass as bass
from concourse import mybir

ALU = mybir.AluOpType
ACT = mybir.ActivationFunctionType
F32 = mybir.dt.float32
BF16 = mybir.dt.bfloat16
I32 = mybir.dt.int32
U32 = mybir.dt.uint32
AX_X = mybir.AxisListType.X

P = 128


def causal_attention_then_top2_experts(
    nc: bass.Bass,
    x: bass.AP, w_attn: bass.AP, b_attn: bass.AP, la_attn: bass.AP, lb_attn: bass.AP,
    w_proj: bass.AP, b_proj: bass.AP, la_proj: bass.AP, lb_proj: bass.AP,
    router_w: bass.AP, gate_proj: bass.AP, up_proj: bass.AP, down_proj: bass.AP,
    out: bass.AP, parts_scratch: bass.AP, rows_scratch: bass.AP, chosen_scratch: bass.AP,
):
    B, T, C = x.shape
    H = 16
    D = C // H
    LORA_R = la_attn.shape[0]
    LORA_SCALE = 0.5
    SCALE = float(D) ** -0.5
    EPS = 1e-5
    NEG = -3.0e38
    E = router_w.shape[1]
    F = gate_proj.shape[2]
    TOKENS = B * T
    NT = TOKENS // P
    TB = T // P
    HQ = 4
    QPB = H // HQ
    G = B * QPB
    PARTS = 3
    PRODUCTS = 6
    Q_PARTS = (0, 1, 2, 0, 1, 0)
    K_PARTS = (0, 0, 0, 1, 1, 2)
    HALF = P // 2
    FC = [(c, min(P, F - c)) for c in range(0, F, P)]
    NFC = len(FC)
    REGION = TOKENS + 2 * P
    MAX_TILES = TOKENS // P
    ET = (2 * TOKENS + E * (P - 1)) // P
    ROW = C + 2
    NO_ROW = 1 << 20
    RING = 6
    assert (T, C, D, TB, QPB) == (512, P, 8, 4, 4) and 3 * HALF // 8 == 24

    x_tiles = x.rearrange("b (t p) c -> p (b t) c", p=P)
    out_tiles = out.rearrange("b (t p) c -> p (b t) c", p=P)
    chosen = chosen_scratch.rearrange("(j t p) c -> j p t c", j=2, p=P)

    with ExitStack() as ctx:
        def sb(name, shape, dt=F32):
            return ctx.enter_context(nc.sbuf_tensor(name, shape, dt))

        def pb(name, shape, dt=F32):
            return ctx.enter_context(nc.psum_tensor(name, shape, dt))

        def sem(name):
            return ctx.enter_context(nc.semaphore(name))

        X = sb("X", [P, NT, C])
        WA = sb("WA", [P, 3, C])
        WP = sb("WP", [P, C])
        LB = sb("LB", [P, 4, LORA_R])
        LA = sb("LA", [LORA_R, 2, C])
        lbT = sb("lbT", [LORA_R, 4, P])
        WT = sb("WT", [P, 3, C])
        WPT = sb("WPT", [P, C])
        RW = sb("RW", [P, E])
        bqk = sb("bqk", [P, 2])
        bv_rows = sb("bv_rows", [P, C])
        bp_rows = sb("bp_rows", [P, C])
        identf = sb("identf", [P, P])
        identb = sb("identb", [P, P], BF16)
        before = sb("before", [P, P], BF16)
        onesb = sb("onesb", [P, P], BF16)
        maskb = sb("maskb", [P, HQ, P], BF16)
        blank_k = sb("blank_k", [P, 2, T], BF16)
        blank_q = sb("blank_q", [P, T], BF16)
        early = sb("early", [P, 12 * T])
        xT = early[:, 0:2 * T].rearrange("p (n t) -> p n t", n=2)
        qk = early[:, 2 * T:4 * T].rearrange("p (s t) -> p s t", s=2)
        rest = early[:, 4 * T:6 * T].rearrange("p (s t) -> p s t", s=2)
        parts = early[:, 6 * T:12 * T].bitcast(BF16).rearrange("p (s e t) -> p s e t", s=2, e=PRODUCTS)
        early_taken = [0]

        def reuse(*shape):
            n = 1
            for extent in shape:
                n *= extent
            flat = early[:, early_taken[0]:early_taken[0] + n]
            early_taken[0] += n
            assert early_taken[0] <= 12 * T
            names = "abcd"[:len(shape)]
            return flat.rearrange(f"p ({' '.join(names)}) -> p {' '.join(names)}",
                                  **{name: extent for name, extent in zip(names[1:], shape[1:])})

        Qs = sb("Qs", [P, G, 2, T], BF16)
        Ks = sb("Ks", [P, G, HQ, T], BF16)
        V9 = sb("V9", [P, G, TB, HQ, D + 1])
        vst = sb("vst", [P, 2, TB, HQ, D + 1])
        negm = sb("negm", [P, 2, TB, HQ])
        mrest = sb("mrest", [P, 2, TB, HQ])
        mparts = sb("mparts", [P, 2, TB, HQ, PARTS], BF16)
        mT = sb("mT", [HQ * PARTS, 2, T], BF16)
        PW = [(TB - kb) * P for kb in range(TB)]
        POFF = [HQ * sum(PW[:kb]) for kb in range(TB)]
        Pt = sb("Pt", [P, 2, HQ * sum(PW)])
        pvs = sb("pvs", [P, T])
        rl = sb("rl", [P, TB, HQ])
        Y = reuse(TB, C)
        yT = reuse(T)
        XR = reuse(TB, C)
        stats = sb("stats", [P, TB, 6])
        mv = sb("mv", [P, TB, 2])
        veps = sb("veps", [P, TB])
        rstd = sb("rstd", [P, TB])
        minus_half = sb("minus_half", [P, TB])
        x1T = reuse(T)
        rows = reuse(2, TB, ROW)
        numbers = sb("numbers", [P, 2, NT], I32)
        lanes = sb("lanes", [P, TB, E])
        sc = sb("sc", [P, TB, E])
        top = sb("top", [P, TB, 8])
        topi = sb("topi", [P, TB, 8], U32)
        topf = sb("topf", [P, 2, TB])
        hot = sb("hot", [P, 2, TB, E])
        hots = sb("hots", [P, TB, E], BF16)
        hot_sum = sb("hot_sum", [P, E], BF16)
        carry = sb("carry", [P, E], BF16)
        ranks = sb("ranks", [P, 2, TB, E])
        rank = sb("rank", [P, 2, TB])
        place = sb("place", [P, 2, TB], U32)
        gap = sb("gap", [P, TB])
        egap = sb("egap", [P, TB])
        steps16 = sb("steps16", [P, E, MAX_TILES])
        over = reuse(E, MAX_TILES)
        count = sb("count", [P, E])
        ntiles = sb("ntiles", [P, E])
        lower = sb("lower", [P, E, E])
        prod8 = reuse(E, E)
        ends = sb("ends", [P, E])
        tile_no = sb("tile_no", [P, ET, E])
        past = reuse(ET, E)
        pastn = reuse(ET, E)
        expert_f = sb("expert_f", [P, ET])
        first_f = sb("first_f", [P, ET])
        behind = sb("behind", [P, ET])
        expert_of = sb("expert_of", [P, ET], I32)
        row_of = sb("row_of", [P, ET], I32)
        fill_f = sb("fill_f", [P, E])
        fill_row = sb("fill_row", [P, E], I32)
        region_f = sb("region_f", [P, E])
        fill = sb("fill", [P, 2, ROW])
        free = Ks[:, :, :, :].rearrange("p g h t -> p (g h t)").bitcast(F32)
        GUW = free[:, 0:2 * E * F].rearrange("p (e w f) -> p e w f", e=E, w=2)
        DW = free[:, 2 * E * F:2 * E * F + E * NFC * C].rearrange("p (e k c) -> p e k c", e=E, k=NFC)
        free_p = Pt[:, :, :].rearrange("p n t -> p (n t)")
        taken = [0]

        def take(n):
            taken[0] += n
            return free_p[:, taken[0] - n:taken[0]]

        xg = take(RING * ROW).rearrange("p (n c) -> p n c", n=RING)
        xgT = take(2 * P).rearrange("p (n t) -> p n t", n=2)
        sg = take(2 * F).rearrange("p (n f) -> p n f", n=2)
        hid = take(2 * F).rearrange("p (n f) -> p n f", n=2)
        hT = take(2 * NFC * P).rearrange("p (n k t) -> p n k t", n=2, k=NFC)
        ys = take(3 * C).rearrange("p (n c) -> p n c", n=3)
        back = take(2 * 2 * TB * C).rearrange("p (n j t c) -> p n j t c", n=2, j=2, t=TB)

        slot = [pb(f"slot{i}", [P, 2 * T]) for i in range(3)]
        pvo = pb("pvo", [P, T])
        misc = pb("misc", [P, T])
        miscb = misc[:, :].bitcast(BF16)

        w_loaded, late_loaded = sem("w_loaded"), sem("late_loaded")
        x_loaded = [sem(f"x_loaded{b}") for b in range(B)]
        consts_ready, ident_ready, ident0 = sem("consts_ready"), sem("ident_ready"), sem("ident0")
        blanks_ready, blanked = sem("blanks_ready"), sem("blanked")
        weights_full, weights_out = sem("weights_full"), sem("weights_out")
        xT_full, xT_out = sem("xT_full"), sem("xT_out")
        q_full, k_full, v_full = sem("q_full"), sem("k_full"), sem("v_full")
        q_out, k_out, v_out = sem("q_out"), sem("k_out"), sem("v_out")
        qsplit, ksplit, qchain, kchain = sem("qsplit"), sem("ksplit"), sem("qchain"), sem("kchain")
        parts_stored = [[sem(f"parts_stored{s}{b}") for b in range(B)] for s in range(2)]
        stacks_loaded = [sem(f"stacks_loaded{b}") for b in range(B)]
        scores_for_max, max_done = sem("scores_for_max"), sem("max_done")
        scores_for_exp, exp_done = sem("scores_for_exp"), sem("exp_done")
        mchain, mparts_ready = sem("mchain"), sem("mparts_ready")
        mT_full, mT_copied = sem("mT_full"), sem("mT_copied")
        maxrows = [sem("maxrows0"), sem("maxrows1")]
        selected, vst_ready = sem("selected"), sem("vst_ready")
        pv_done, pvs_copied = sem("pv_done"), sem("pvs_copied")
        yT_full, rl_ready, y_done = sem("yT_full"), sem("rl_ready"), sem("y_done")
        pool_passed, dve_passed = sem("pool_passed"), sem("dve_passed")
        xb_ready, lists_ready = sem("xb_ready"), sem("lists_ready")
        fT_full, fT_out, proj_full = sem("fT_full"), sem("fT_out"), sem("proj_full")
        dchain = sem("dchain")
        stats_ready, veps_ready, rstd_ready = sem("stats_ready"), sem("veps_ready"), sem("rstd_ready")
        x1_ready, x1T_full, x1T_out, rows_copied = sem("x1_ready"), sem("x1T_full"), sem("x1T_out"), sem("rows_copied")
        router_full, hot_ready, gap_ready, egap_ready = sem("router_full"), sem("hot_ready"), sem("gap_ready"), sem("egap_ready")
        prefix_full, place_ready, numbered, scattered = sem("prefix_full"), sem("place_ready"), sem("numbered"), sem("scattered")
        fills_ready, tables_ready, filled = sem("fills_ready"), sem("tables_ready"), sem("filled")
        experts_loaded = sem("experts_loaded")
        xg_loaded = [sem(f"xg_loaded{i}") for i in range(RING)]
        xgT_full, xgT_ready = sem("xgT_full"), sem("xgT_ready")
        gu_full, silu_done, h_ready = sem("gu_full"), sem("silu_done"), sem("h_ready")
        hT_full, hT_ready, y_full, ys_ready = sem("hT_full"), sem("hT_ready"), sem("y_full"), sem("ys_ready")
        y_scattered = [sem(f"y_scattered{i}") for i in range(RING)]
        back_loaded = [sem(f"back_loaded{i}") for i in range(B)]
        first_added, both_added, norm2, out_stored = sem("first_added"), sem("both_added"), sem("norm2"), sem("out_stored")

        S_UNITS = [(3, 0, 2), (3, 2, 2), (2, 0, 2), (2, 2, 2), (1, 0, 4), (0, 0, 4)]
        T_UNITS = [(0, 0, 2), (0, 2, 2), (1, 0, 2), (1, 2, 2), (2, 0, 4), (3, 0, 4)]
        NU = len(S_UNITS)

        def s_view(u, n):
            qb, _, heads = S_UNITS[u]
            return slot[n][:, :].rearrange("p (h k) -> p h k", k=[128, 256, 512, 512][qb])[:, 0:heads, 0:(qb + 1) * P]

        def t_view(u, n):
            kb, _, heads = T_UNITS[u]
            return slot[n][:, :].rearrange("p (h k) -> p h k", k=[512, 512, 256, 128][kb])[:, 0:heads, 0:PW[kb]]

        def p_view(par, kb):
            return Pt[:, par, POFF[kb]:POFF[kb] + HQ * PW[kb]].rearrange("p (h q) -> p h q", h=HQ)

        def number_column(j):
            return rows[:, j, :, C:C + 1].rearrange("p t a -> p (t a)").bitcast(I32)

        W_DMAS = 5
        LATE_DMAS = 4
        STACK_DMAS = 2 * 2 * PRODUCTS * 16
        LOOP_FROM = 8

        def expert_steps(eng, step):
            for s in range(LOOP_FROM):
                step(s, s % RING)
            with eng.Fori(0, (ET - 1 - LOOP_FROM) // RING) as i:
                for r in range(RING):
                    step(RING * i + (LOOP_FROM + r), (LOOP_FROM + r) % RING)
            for s in range(LOOP_FROM + (ET - 1 - LOOP_FROM) // RING * RING, ET + 2):
                step(s, s % RING)

        block = ctx.enter_context(nc.Block())

        @block.sync
        def _(sp):
            sp.dma_start(X[:, 0:TB, :], x_tiles[:, 0:TB, :]).then_inc(x_loaded[0], 16)
            sp.dma_start(WA[:, :, :], w_attn.rearrange("(j p) c -> p j c", p=P)).then_inc(w_loaded, 16)
            sp.dma_start(LB[:, 0:3, :], lb_attn.rearrange("(j p) r -> p j r", p=P)).then_inc(w_loaded, 16)
            sp.dma_start(LB[:, 3, :], lb_proj).then_inc(w_loaded, 16)
            sp.dma_start(LA[:, 0, :], la_attn).then_inc(w_loaded, 16)
            sp.dma_start(bqk[:, :], b_attn[0:2 * C].rearrange("(j p) -> p j", p=P), allow_slow_non_contiguous=True).then_inc(w_loaded, 16)
            for b in range(1, B):
                sp.dma_start(X[:, b * TB:(b + 1) * TB, :], x_tiles[:, b * TB:(b + 1) * TB, :]).then_inc(x_loaded[b], 16)
            for b in range(B):
                for s, split in ((0, qsplit), (1, ksplit)):
                    sp.wait_ge(split, b + 1)
                    sp.dma_start(parts_scratch[b, s], parts[:, s].rearrange("p e t -> p (e t)")).then_inc(parts_stored[s][b], 16)
                sp.wait_ge(blanked, b + 1)
                for s in range(2):
                    sp.wait_ge(parts_stored[s][b], 16)
                    src = parts_scratch[b, s].rearrange("(j a d) (e t) -> a e d j t", a=2, d=D, e=PRODUCTS)
                    for a in range(2):
                        for e in range(PRODUCTS):
                            row = HALF * a + PARTS + D * e
                            if s == 0:
                                dst = Qs[row:row + D, QPB * b:QPB * (b + 1)].rearrange("p g c t -> p (g c) t")
                            else:
                                dst = Ks[row:row + D, QPB * b:QPB * (b + 1)].rearrange("p g (c a) t -> p a (g c) t", a=2)[:, a]
                            sp.dma_start(dst, src[a, e]).then_inc(stacks_loaded[b], 16)

            def store_maxrows(g, par):
                sp.wait_ge(mT_copied, g + 1)
                for h in range(HQ):
                    sp.dma_start(Qs[HALF * (h % 2):HALF * (h % 2) + PARTS, bass.ds(g, 1), h // 2, :],
                                 mT[PARTS * h:PARTS * (h + 1), par, :]).then_inc(maxrows[par], 16)

            store_maxrows(0, 0)
            store_maxrows(1, 1)
            with sp.Fori(1, G // 2) as pair:
                store_maxrows(2 * pair, 0)
                store_maxrows(2 * pair + 1, 1)
            sp.wait_ge(scores_for_exp, NU * G)
            for w, src in enumerate((gate_proj, up_proj)):
                sp.dma_start(GUW[:, :, w, :], src.rearrange("e d f -> d e f")).then_inc(experts_loaded, 16)
            for k, (f0, fn) in enumerate(FC):
                sp.dma_start(DW[0:fn, :, k, :], down_proj[:, f0:f0 + fn, :].rearrange("e f c -> f e c")).then_inc(experts_loaded, 16)
            sp.wait_ge(fills_ready, 1)
            for e in range(0, E, 2):
                at = sp.value_load(fill_row[0:1, e:e + 1], min_val=e * REGION, max_val=e * REGION + TOKENS)
                sp.dma_start(rows_scratch[bass.ds(at, 2 * P), :].rearrange("(p a) c -> p (a c)", a=2),
                             fill[:, :, :].rearrange("p a c -> p (a c)")).then_inc(filled, 16)
            sp.wait_ge(tables_ready, 1)
            sp.wait_ge(scattered, 16 + 2 * TB * B * 16)
            sp.wait_ge(filled, 16 * E)

            def load_rows(j, ring, index=None):
                at = sp.value_load(row_of[0:1, bass.ds(j, 1)], min_val=0, max_val=E * REGION - P)
                sp.dma_start(xg[:, ring, :], rows_scratch[bass.ds(at, P), :]).then_inc(xg_loaded[ring], 16)

            sp.wait_ge(pv_done, G)
            for j in range(RING):
                load_rows(j, j)
            with sp.Fori(1, ET // RING) as i:
                for r in range(RING):
                    sp.wait_ge(y_scattered[r], 16 * i)
                    load_rows(RING * i + r, r)
            for j in range(ET // RING * RING, ET):
                sp.wait_ge(y_scattered[j % RING], 16 * (j // RING))
                load_rows(j, j % RING)
            for r in range(RING):
                sp.wait_ge(y_scattered[r], 16 * len(range(r, ET, RING)))
            for b in range(B):
                if b >= 2:
                    sp.wait_ge(both_added, b - 1)
                for j in range(2):
                    sp.dma_start(back[:, b % 2, j], chosen[j, :, b * TB:(b + 1) * TB, :]).then_inc(back_loaded[b], 16)
            for b in range(B):
                sp.wait_ge(norm2, b + 1)
                sp.dma_start(out_tiles[:, b * TB:(b + 1) * TB, :], X[:, b * TB:(b + 1) * TB, :]).then_inc(out_stored, 16)
            sp.wait_ge(out_stored, 16 * B)

        @block.gpsimd
        def _(pool):
            pool.dma_start(RW[:, :], router_w).then_inc(scattered, 16)
            pool.memset(identf[:, :], 0.0).then_inc(ident0, 1)
            pool.memset(maskb[:, :, :], 0.0).then_inc(ident0, 1)
            pool.wait_ge(ident0, 2)
            pool.affine_select(out=identf[:, :], in_=identf[:, :], compare_op=ALU.not_equal, fill=1.0,
                               base=0, pattern=[[-1, P]], channel_multiplier=1).then_inc(ident_ready, 1)
            pool.affine_select(out=maskb[:, :, :], in_=maskb[:, :, :], compare_op=ALU.is_ge, fill=NEG,
                               base=0, pattern=[[0, HQ], [-1, P]], channel_multiplier=1).then_inc(consts_ready, 1)
            pool.wait_ge(ident_ready, 1)
            pool.tensor_copy(identb[:, :], identf[:, :]).then_inc(consts_ready, 1)
            n = 0
            for b in range(B):
                pool.wait_ge(k_out, 2 * (b + 1))
                pool.tensor_tensor(rest[:, 1, :], qk[:, 1, :], parts[:, 1, 0, :], ALU.subtract).then_inc(kchain, 1)
                pool.tensor_copy(parts[:, 1, 1, :], parts[:, 1, 0, :])
                pool.tensor_copy(parts[:, 1, 2, :], parts[:, 1, 0, :])
                pool.wait_ge(kchain, 2 * b + 1)
                pool.tensor_copy(parts[:, 1, 3, :], rest[:, 1, :]).then_inc(kchain, 1)
                pool.tensor_copy(parts[:, 1, 4, :], rest[:, 1, :])
                pool.wait_ge(kchain, 2 * b + 2)
                pool.tensor_tensor(parts[:, 1, 5, :], rest[:, 1, :], parts[:, 1, 3, :], ALU.subtract).then_inc(ksplit, 1)
                if b == 0:
                    pool.memset(carry[:, :], 0.0)
                    pool.memset(minus_half[:, :], -0.5)
                    pool.memset(onesb[:, :], 1.0).then_inc(ident0, 1)
                    pool.wait_ge(ident0, 3)
                    pool.affine_select(out=before[:, :], in_=onesb[:, :], compare_op=ALU.is_gt, fill=0.0,
                                       base=0, pattern=[[1, P]], channel_multiplier=-1)
                    pool.iota(lanes[:, :, :], pattern=[[0, TB], [1, E]], base=0, channel_multiplier=0,
                              allow_small_or_imprecise_dtypes=True)
                    pool.iota(numbers[:, :, :], pattern=[[TOKENS, 2], [P, NT]], base=0, channel_multiplier=1)
                    pool.iota(steps16[:, :, :], pattern=[[0, E], [P, MAX_TILES]], base=0, channel_multiplier=0,
                              allow_small_or_imprecise_dtypes=True)
                    pool.iota(tile_no[:, :, :], pattern=[[1, ET], [0, E]], base=0, channel_multiplier=0,
                              allow_small_or_imprecise_dtypes=True)
                    pool.iota(region_f[:, :], pattern=[[REGION, E]], base=0, channel_multiplier=0,
                              allow_small_or_imprecise_dtypes=True)
                    pool.memset(lower[:, :, :], 1.0).then_inc(ident0, 1)
                    pool.wait_ge(ident0, 4)
                    pool.affine_select(out=lower[:, :, :], in_=lower[:, :, :], compare_op=ALU.is_ge, fill=0.0,
                                       base=0, pattern=[[1, E], [-1, E]], channel_multiplier=0)
                    pool.memset(fill[:, :, :], 0.0).then_inc(ident0, 1)
                    pool.wait_ge(ident0, 5)
                    pool.memset(fill[:, :, C:C + 1].bitcast(I32), NO_ROW).then_inc(lists_ready, 1)
            pool.wait_ge(xT_full, B)
            pool.wait_ge(late_loaded, 16 * LATE_DMAS)
            for t in range(NT):
                last = pool.tensor_tensor(X[:, t, :], X[:, t, :], bp_rows[:, :], ALU.add)
            last.then_inc(xb_ready, 1)

            def wait_counted(semaphore, count_):
                pool.wait_ge(semaphore, count_)
                pool.sem_inc(pool_passed, 1)

            def split_max(g, par):
                wait_counted(max_done, NU * g + NU)
                if not isinstance(g, int) or g >= 2:
                    wait_counted(mT_full, g - 1)
                m = negm[:, par]
                r = mrest[:, par]
                p = [mparts[:, par, :, :, e] for e in range(PARTS)]
                pool.tensor_copy(p[0], m).then_inc(mchain, 1)
                pool.wait_ge(mchain, 3 * g + 1)
                pool.tensor_tensor(r, m, p[0], ALU.subtract).then_inc(mchain, 1)
                wait_counted(mchain, 3 * g + 2)
                pool.tensor_copy(p[1], r).then_inc(mchain, 1)
                pool.wait_ge(mchain, 3 * g + 3)
                pool.tensor_tensor(p[2], r, p[1], ALU.subtract).then_inc(mparts_ready, 1)

            def select(g, par, kb):
                wait_counted(exp_done, NU * g + [2, 4, 5, 6][kb])
                v = p_view(par, kb)[:, :, 0:P]
                pool.affine_select(out=v, in_=v, compare_op=ALU.is_ge, fill=0.0, base=0,
                                   pattern=[[0, HQ], [1, P]], channel_multiplier=-1).then_inc(selected, 1)

            def inverse_deviation(b):
                wait_counted(stats_ready, b + 1)
                pool.tensor_scalar(veps[:, :], mv[:, :, 1], EPS, None, ALU.add).then_inc(veps_ready, 1)
                pool.wait_ge(veps_ready, b + 1)
                pool.tensor_tensor(rstd[:, :], veps[:, :], minus_half[:, :], ALU.pow).then_inc(rstd_ready, 1)

            def number_rows(b):
                wait_counted(scattered, 16 + 2 * TB * 16 * b)
                for j in range(2):
                    last = pool.tensor_copy(number_column(j), numbers[:, j, bass.ds(b * TB, TB)])
                last.then_inc(numbered, 1)

            def scatter_rows(b):
                wait_counted(place_ready, b + 1)
                wait_counted(rows_copied, 2 * b + 2)
                wait_counted(numbered, b + 1)
                for j in range(2):
                    for t in range(TB):
                        pool.indirect_dma_start(rows_scratch, bass.IndirectOffsetOnAxis(place[:, j, t:t + 1], 0),
                                                rows[:, j, t, :], None).then_inc(scattered, 16)

            def step(g, k, end=None, scores=True, exps=True):
                par = k % 2
                if exps:
                    if not isinstance(g, int) or g >= 2:
                        wait_counted(pv_done, g - 1)
                    pool.tensor_copy(vst[:, par].rearrange("p t h d -> p (t h d)"),
                                     V9[:, bass.ds(g, 1)].rearrange("p g t h d -> p (g t h d)")).then_inc(vst_ready, 1)
                if end is not None and k == 3:
                    inverse_deviation(end)
                for kb in range(TB):
                    if exps:
                        select(g, par, kb)
                    if kb == 1 and end is not None and k == 3:
                        number_rows(end)
                if scores:
                    split_max(g + 2, par)
                if end is not None and k == 3:
                    scatter_rows(end)

            split_max(0, 0)
            split_max(1, 1)
            pool.wait_ge(v_out, B)
            step(0, 2)
            step(1, 3)
            with pool.Fori(0, B - 1) as b:
                for k in range(4):
                    step(4 * b + 2 + k, k, end=b)
            step(14, 0, scores=False)
            step(15, 1, scores=False)
            inverse_deviation(B - 1)
            number_rows(B - 1)
            scatter_rows(B - 1)

            def scatter_results(j, ring):
                wait_counted(ys_ready, j + 1)
                pool.indirect_dma_start(chosen_scratch, bass.IndirectOffsetOnAxis(xg[:, ring, C:C + 1].bitcast(U32), 0),
                                        ys[:, ring % 3, :], None, bounds_check=2 * TOKENS - 1,
                                        oob_is_err=False).then_inc(y_scattered[ring], 16)

            with pool.Fori(0, ET // RING) as i:
                for r in range(RING):
                    scatter_results(RING * i + r, r)
            for j in range(ET // RING * RING, ET):
                scatter_results(j, j % RING)

            for b in range(B):
                pool.wait_ge(back_loaded[b], 32)
                xb = X[:, b * TB:(b + 1) * TB, :].rearrange("p t c -> p (t c)")
                pool.tensor_tensor(xb, xb, back[:, b % 2, 0].rearrange("p t c -> p (t c)"), ALU.add).then_inc(first_added, 1)
                if b:
                    inverse_deviation(B + b - 1)
            inverse_deviation(2 * B - 1)

        @block.scalar
        def _(act):
            for dst, src in ((LA[:, 1, :], la_proj), (WP[:, :], w_proj),
                             (bv_rows[:, :], b_attn[2 * C:3 * C].rearrange("(a c) -> a c", a=1).broadcast_to([P, C])),
                             (bp_rows[:, :], b_proj.rearrange("(a c) -> a c", a=1).broadcast_to([P, C]))):
                act.dma_start(dst, src).then_inc(late_loaded, 16)
            for b in range(B):
                act.wait_ge(xT_full, b + 1)
                if b >= 2:
                    act.wait_ge(v_full, b - 1)
                act.activation(xT[:, b % 2, :], misc[:, :], ACT.Copy).then_inc(xT_out, 1)
                for s, full, split, done in ((0, q_full, qsplit, q_out), (1, k_full, ksplit, k_out)):
                    act.wait_ge(full, b + 1)
                    if b == 0:
                        act.wait_ge(w_loaded, 16 * W_DMAS)
                    else:
                        act.wait_ge(parts_stored[s][b - 1], 16)
                    src = slot[0][:, s * T:(s + 1) * T]
                    act.activation(parts[:, s, 0, :], src, ACT.Identity, bias=bqk[:, s:s + 1]).then_inc(done, 1)
                    act.activation(qk[:, s, :], src, ACT.Identity, bias=bqk[:, s:s + 1]).then_inc(done, 1)

            def copy_mT(g, par):
                act.wait_ge(mT_full, g + 1)
                act.activation(mT[:, par, :], miscb[0:HQ * PARTS, 0:T], ACT.Copy).then_inc(mT_copied, 1)

            def copy_pv(g):
                act.wait_ge(pv_done, g + 1)
                if not isinstance(g, int) or g >= 1:
                    act.wait_ge(yT_full, g)
                act.activation(pvs[:, :], pvo[:, :], ACT.Copy).then_inc(pvs_copied, 1)

            def copy_yT(b):
                act.wait_ge(fT_full, b + 1)
                act.activation(yT[:, :], misc[:, :], ACT.Copy).then_inc(fT_out, 1)

            def copy_x1(b):
                act.wait_ge(x1T_full, b + 1)
                act.activation(x1T[:, :], misc[:, :], ACT.Copy).then_inc(x1T_out, 1)
                act.activation(rows[:, 1, :, 0:C], rows[:, 0, :, 0:C], ACT.Copy).then_inc(rows_copied, 1)
                act.activation(X[:, bass.ds(b * TB, TB), :], rows[:, 0, :, 0:C], ACT.Copy).then_inc(rows_copied, 1)

            def exp_gap(b):
                act.wait_ge(gap_ready, b + 1)
                act.activation(egap[:, :], gap[:, :], ACT.Exp).then_inc(egap_ready, 1)

            def step(g, k, end=None, exps=True, pv=True, maxrows=True):
                par = k % 2
                for u in range(NU):
                    if exps:
                        kb, h0, heads = T_UNITS[u]
                        act.wait_ge(scores_for_exp, NU * g + u + 1)
                        if u == 0 and (not isinstance(g, int) or g >= 2):
                            act.wait_ge(pv_done, g - 1)
                        act.activation(p_view(par, kb)[:, h0:h0 + heads, :], t_view(u, (2 * u + 1) % 3), ACT.Exp,
                                       scale=SCALE).then_inc(exp_done, 1)
                    if u == 1 and maxrows:
                        copy_mT(g + 1, 1 - par)
                    if u == 2 and pv:
                        copy_pv(g - 1)
                    if u == 3 and end is not None and k == 3:
                        copy_x1(end)
                    if u == 4 and end is not None and k == 2:
                        copy_yT(end)
                    if u == 5 and end is not None and k == 3:
                        exp_gap(end)

            copy_mT(0, 0)
            step(0, 2, pv=False)
            step(1, 3)
            with act.Fori(0, B - 1) as b:
                for k in range(4):
                    step(4 * b + 2 + k, k, end=b)
            step(14, 0)
            step(15, 1, maxrows=False)
            copy_pv(15)
            copy_yT(B - 1)
            copy_x1(B - 1)
            exp_gap(B - 1)
            act.wait_ge(fills_ready, 1)
            for e in range(1, E, 2):
                at = act.value_load(fill_row[0:1, e:e + 1], min_val=e * REGION, max_val=e * REGION + TOKENS)
                act.dma_start(rows_scratch[bass.ds(at, 2 * P), :].rearrange("(p a) c -> p (a c)", a=2),
                              fill[:, :, :].rearrange("p a c -> p (a c)")).then_inc(filled, 16)

            def silu(s, two):
                act.wait_ge(gu_full, s + 1)
                if not isinstance(s, int) or s >= 2:
                    act.wait_ge(h_ready, s - 1)
                act.activation(sg[:, two, :], slot[two][:, 0:F], ACT.Silu).then_inc(silu_done, 1)

            def weigh(j, ring, freed):
                act.wait_ge(y_full, j + 1)
                if freed is not None:
                    act.wait_ge(y_scattered[(ring - 3) % RING], freed)
                act.activation(ys[:, ring % 3, :], pvo[:, 0:C], ACT.Copy, scale=xg[:, ring, C + 1:C + 2]).then_inc(ys_ready, 1)

            def expert_step(s, m, i=None):
                if not isinstance(s, int) or s < ET:
                    silu(s, m % 2)
                if not isinstance(s, int) or s >= 2:
                    j = s - 2
                    ring = (m - 2) % RING
                    if isinstance(s, int):
                        freed = 16 * ((j - 3) // RING + 1) if j >= 3 else None
                    else:
                        freed = 16 * ((j - 3 - (ring - 3) % RING) // RING + 1)
                    weigh(j, ring, freed)

            expert_steps(act, expert_step)

        @block.vector
        def _(dve):
            chain = [0]

            def link(instruction, carried=False):
                instruction.then_inc(dchain, 1)
                chain[0] += 1
                if loop[0] is None:
                    dve.wait_ge(dchain, chain[0])
                else:
                    dve.wait_ge(dchain, loop[0] * LINKS + chain[0])
                    if carried:
                        dve.sem_inc(dve_passed, 1)

            loop = [None]
            LINKS = 12

            dve.memset(blank_k[:, :, :].rearrange("p a t -> p (a t)").bitcast(F32), 0.0)
            dve.memset(blank_q[:, :].bitcast(F32), 0.0).then_inc(blanks_ready, 1)
            dve.wait_ge(blanks_ready, 1)
            for a in range(2):
                last = dve.memset(blank_k[HALF * a:HALF * a + PARTS, a, :], 1.0)
            last.then_inc(blanks_ready, 1)
            dve.wait_ge(blanks_ready, 2)

            def blank(b):
                for c in range(2):
                    dve.tensor_copy(Ks[:, QPB * b:QPB * (b + 1), 2 * c:2 * c + 2, :].rearrange("p g h t -> p g (h t)"),
                                    blank_k[:, :, :].rearrange("p (o a) t -> p o (a t)", o=1).broadcast_to([P, QPB, 2 * T]))
                dve.tensor_copy(Qs[:, QPB * b:QPB * (b + 1)].rearrange("p g c t -> p (g c) t"),
                                blank_q[:, :].rearrange("p (o t) -> p o t", o=1).broadcast_to([P, 2 * QPB, T])).then_inc(blanked, 1)

            blank(0)
            dve.memset(pvo[:, :], 0.0)
            dve.memset(V9[:, :, :, :, D:D + 1], 1.0)
            dve.wait_ge(weights_full, 1)
            dve.tensor_scalar(lbT[:, :, :].rearrange("r j p -> r (j p)"), slot[1][0:LORA_R, 0:T], LORA_SCALE, None,
                              ALU.mult).then_inc(weights_out, 1)
            dve.wait_ge(weights_full, 2)
            dve.tensor_copy(WT[:, :, :].rearrange("p j c -> p (j c)"), slot[2][:, 0:3 * C]).then_inc(weights_out, 1)
            for b in range(B):
                dve.wait_ge(q_out, 2 * (b + 1))
                dve.tensor_tensor(rest[:, 0, :], qk[:, 0, :], parts[:, 0, 0, :], ALU.subtract).then_inc(qchain, 1)
                dve.tensor_copy(parts[:, 0, 3, :], parts[:, 0, 0, :])
                dve.wait_ge(qchain, 2 * b + 1)
                dve.tensor_copy(parts[:, 0, 1, :], rest[:, 0, :]).then_inc(qchain, 1)
                dve.tensor_copy(parts[:, 0, 5, :], parts[:, 0, 0, :])
                dve.wait_ge(qchain, 2 * b + 2)
                dve.tensor_tensor(parts[:, 0, 2, :], rest[:, 0, :], parts[:, 0, 1, :], ALU.subtract)
                dve.tensor_copy(parts[:, 0, 4, :], parts[:, 0, 1, :]).then_inc(qsplit, 1)
                dve.wait_ge(v_full, b + 1)
                if b == 0:
                    dve.wait_ge(late_loaded, 16 * LATE_DMAS)
                for t in range(TB):
                    last = dve.tensor_tensor(V9[:, QPB * b:QPB * (b + 1), t, :, 0:D],
                                             slot[1][:, T + t * C:T + (t + 1) * C].rearrange("p (i h d) -> p i h d", i=QPB, h=HQ),
                                             bv_rows[:, :].rearrange("p (i h d) -> p i h d", i=QPB, h=HQ), ALU.add)
                last.then_inc(v_out, 1)
                if b == 0:
                    dve.wait_ge(weights_full, 3)
                    dve.tensor_copy(WPT[:, :], slot[2][:, T:T + C]).then_inc(weights_out, 1)
                if b + 1 < B:
                    blank(b + 1)

            def row_max(g, par, u, n):
                qb, h0, heads = S_UNITS[u]
                dve.wait_ge(scores_for_max, NU * g + u + 1)
                if u == 0 and (not isinstance(g, int) or g >= 2):
                    dve.wait_ge(mparts_ready, g - 1)
                dve.tensor_reduce(negm[:, par, qb, h0:h0 + heads], s_view(u, n), AX_X, ALU.max,
                                  negate=True).then_inc(max_done, 1)

            def normalize(g, i):
                dve.wait_ge(yT_full, g + 1)
                v = misc[:, :].rearrange("p (t h e) -> p t h e", t=TB, h=HQ)
                dve.reciprocal(rl[:, :, :], v[:, :, :, D]).then_inc(rl_ready, 1)
                dve.wait_ge(rl_ready, g + 1)
                dve.tensor_tensor(Y[:, :, i * HQ * D:(i + 1) * HQ * D].rearrange("p t (h d) -> p t h d", h=HQ), v[:, :, :, 0:D],
                                  rl[:, :, :].rearrange("p t (h a) -> p t h a", a=1).broadcast_to([P, TB, HQ, D]),
                                  ALU.mult).then_inc(y_done, 1)

            def statistics(src, done):
                for t in range(TB):
                    last = dve.bn_stats(stats[:, t, :], src[:, t, :])
                link(last, carried=True)
                for t in range(TB):
                    last = dve.bn_aggr(mv[:, t, :], stats[:, t, :])
                last.then_inc(done, 1)

            def residual(b):
                dve.wait_ge(proj_full, b + 1)
                link(dve.tensor_tensor(XR[:, :, :].rearrange("p t c -> p (t c)"), misc[:, :],
                                       X[:, bass.ds(b * TB, TB), :].rearrange("p t c -> p (t c)"), ALU.add))
                statistics(XR, stats_ready)

            def normed(b):
                dve.wait_ge(rstd_ready, b + 1)
                dve.wait_ge(scattered, 16 + 2 * TB * 16 * b)
                for t in range(TB):
                    last = dve.tensor_scalar(rows[:, 0, t, 0:C], XR[:, t, :], mv[:, t, 0:1], rstd[:, t:t + 1],
                                             ALU.subtract, ALU.mult)
                last.then_inc(x1_ready, 1)

            def choose(b):
                dve.wait_ge(router_full, b + 1)
                link(dve.tensor_copy(sc[:, :, :].rearrange("p t e -> p (t e)"), misc[:, 0:TB * E]), carried=True)
                for t in range(TB):
                    last = dve.max(top[:, t, :], sc[:, t, :])
                link(last, carried=True)
                for t in range(TB):
                    last = dve.max_index(topi[:, t, :], top[:, t, :], sc[:, t, :])
                dve.tensor_tensor(gap[:, :], top[:, :, 1], top[:, :, 0], ALU.subtract).then_inc(gap_ready, 1)
                link(last)
                link(dve.tensor_copy(topf[:, :, :].rearrange("p j t -> p t j"), topi[:, :, 0:2]))
                for j in range(2):
                    last = dve.tensor_tensor(hot[:, j], lanes[:, :, :],
                                             topf[:, j, :].rearrange("p (t a) -> p t a", a=1).broadcast_to([P, TB, E]), ALU.is_equal)
                link(last)
                link(dve.tensor_tensor(hots[:, :, :], hot[:, 0], hot[:, 1], ALU.add))
                with nc.allow_low_precision(reason="counts up to four are exact in bf16"):
                    dve.tensor_reduce(hot_sum[:, :], hots[:, :, :].rearrange("p t e -> p e t"), AX_X, ALU.add).then_inc(hot_ready, 1)

            def place_rows(b):
                dve.wait_ge(prefix_full, b + 1)
                for j in range(2):
                    last = dve.tensor_tensor(ranks[:, j], hot[:, j], misc[:, 0:TB * E].rearrange("p (t e) -> p t e", e=E), ALU.mult)
                link(last)
                if isinstance(b, int):
                    dve.tensor_copy(count[:, :], misc[:, TB * E:TB * E + E])
                link(dve.tensor_reduce(rank[:, :, :], ranks[:, :, :, :], AX_X, ALU.add))
                dve.tensor_tensor(carry[:, :], carry[:, :], hot_sum[:, :], ALU.add)
                dve.wait_ge(egap_ready, b + 1)
                link(dve.tensor_scalar(gap[:, :], egap[:, :], 1.0, None, ALU.add))
                link(dve.reciprocal(gap[:, :], gap[:, :]))
                dve.tensor_copy(rows[:, 0, :, C + 1], gap[:, :])
                dve.tensor_tensor(rows[:, 1, :, C + 1], gap[:, :], egap[:, :], ALU.mult)
                dve.scalar_tensor_tensor(out=place[:, :, :], in0=topf[:, :, :], scalar=float(REGION), in1=rank[:, :, :],
                                         op0=ALU.mult, op1=ALU.add).then_inc(place_ready, 1)

            def step(g, k, end=None, scores=True, pv=True):
                par = k % 2
                for u in range(NU):
                    if scores:
                        row_max(g + 2, par, u, (2 * u) % 3)
                    if end is not None and k == 3:
                        if u == 0:
                            residual(end)
                        if u == 1:
                            normed(end)
                        if u == 4:
                            choose(end)
                    if u == (4 if k == 3 else 3) and pv:
                        normalize(g - 1, (k + 1) % 4)
                    if end is not None and k == 3 and u == 5:
                        place_rows(end)

            for g in range(2):
                for u in range(NU):
                    row_max(g, g, u, (NU * g + u) % 3)
            step(0, 2, pv=False)
            for s in range(2):
                dve.wait_ge(parts_stored[s][B - 1], 16)
            step(1, 3)
            dve.wait_ge(xb_ready, 1)
            dve.wait_ge(lists_ready, 1)
            with dve.Fori(0, B - 1) as b:
                loop[0] = b
                chain[0] = 0
                for k in range(4):
                    step(4 * b + 2 + k, k, end=b)
                assert chain[0] == LINKS, chain[0]
            loop[0] = None
            chain[0] = LINKS * (B - 1)
            step(14, 0, scores=False)
            step(15, 1, scores=False)
            normalize(15, 3)
            residual(B - 1)
            normed(B - 1)
            choose(B - 1)
            place_rows(B - 1)

            link(dve.tensor_tensor(fill_f[:, :], count[:, :], region_f[:, :], ALU.add))
            dve.tensor_copy(fill_row[:, :], fill_f[:, :]).then_inc(fills_ready, 1)
            link(dve.tensor_tensor(over[:, :, :], count[:, :].rearrange("p (e a) -> p e a", a=1).broadcast_to([P, E, MAX_TILES]),
                                   steps16[:, :, :], ALU.is_gt))
            link(dve.tensor_reduce(ntiles[:, :], over[:, :, :], AX_X, ALU.add))
            link(dve.tensor_tensor(prod8[:, :, :], lower[:, :, :], ntiles[:, :].rearrange("p (a e) -> p a e", a=1).broadcast_to([P, E, E]), ALU.mult))
            link(dve.tensor_reduce(ends[:, :], prod8[:, :, :], AX_X, ALU.add))
            link(dve.tensor_tensor(past[:, :, :], tile_no[:, :, :], ends[:, :].rearrange("p (a e) -> p a e", a=1).broadcast_to([P, ET, E]), ALU.is_ge))
            link(dve.tensor_tensor(pastn[:, :, :], past[:, :, :], ntiles[:, :].rearrange("p (a e) -> p a e", a=1).broadcast_to([P, ET, E]), ALU.mult))
            dve.tensor_reduce(expert_f[:, :], past[:, :, :], AX_X, ALU.add)
            link(dve.tensor_reduce(first_f[:, :], pastn[:, :, :], AX_X, ALU.add))
            link(dve.tensor_tensor(first_f[:, :], tile_no[:, :, 0], first_f[:, :], ALU.subtract))
            link(dve.tensor_scalar(behind[:, :], first_f[:, :], -1.0, ntiles[:, E - 1:E], ALU.mult, ALU.add))
            link(dve.tensor_tensor(behind[:, :], behind[:, :], past[:, :, E - 1], ALU.mult))
            link(dve.tensor_tensor(first_f[:, :], first_f[:, :], behind[:, :], ALU.add))
            link(dve.tensor_scalar(expert_f[:, :], expert_f[:, :], float(E - 1), None, ALU.min))
            link(dve.tensor_scalar(first_f[:, :], first_f[:, :], float(P), None, ALU.mult))
            dve.tensor_copy(expert_of[:, :], expert_f[:, :])
            dve.scalar_tensor_tensor(out=row_of[:, :], in0=expert_f[:, :], scalar=float(REGION), in1=first_f[:, :],
                                     op0=ALU.mult, op1=ALU.add).then_inc(tables_ready, 1)

            def copy_xT(j, two):
                dve.wait_ge(xgT_full, j + 1)
                if not isinstance(j, int) or j >= 2:
                    dve.wait_ge(gu_full, j - 1)
                dve.tensor_copy(xgT[:, two, :], misc[:, 0:P]).then_inc(xgT_ready, 1)

            def copy_hT(j, two):
                dve.wait_ge(hT_full, j + 1)
                if not isinstance(j, int) or j >= 2:
                    dve.wait_ge(y_full, j - 1)
                src = slot[2][:, two * T:two * T + NFC * P]
                dve.tensor_copy(hT[:, two, 0:NFC - 1].rearrange("p k t -> p (k t)"), src[:, 0:(NFC - 1) * P])
                dve.tensor_copy(hT[0:FC[-1][1], two, NFC - 1, :], src[0:FC[-1][1], (NFC - 1) * P:NFC * P]).then_inc(hT_ready, 1)

            def hidden(s, two):
                dve.wait_ge(silu_done, s + 1)
                dve.tensor_tensor(hid[:, two, :], slot[two][:, T:T + F], sg[:, two, :], ALU.mult).then_inc(h_ready, 1)

            def expert_step(s, m):
                static = isinstance(s, int)
                if not static or 1 <= s <= ET:
                    copy_hT(s - 1, (m - 1) % 2)
                if not static or s + 1 < ET:
                    copy_xT(s + 1, (m + 1) % 2)
                if not static or s < ET:
                    hidden(s, m % 2)

            copy_xT(0, 0)
            expert_steps(dve, expert_step)
            for b in range(B):
                dve.wait_ge(first_added, b + 1)
                xb = X[:, b * TB:(b + 1) * TB, :].rearrange("p t c -> p (t c)")
                dve.tensor_tensor(xb, xb, back[:, b % 2, 1].rearrange("p t c -> p (t c)"), ALU.add).then_inc(both_added, 1)
                dve.wait_ge(both_added, b + 1)
                statistics(X[:, b * TB:(b + 1) * TB, :], stats_ready)
                dve.wait_ge(rstd_ready, B + b + 1)
                for t in range(TB):
                    tile = X[:, b * TB + t, :]
                    last = dve.tensor_scalar(tile, tile, mv[:, t, 0:1], rstd[:, t:t + 1], ALU.subtract, ALU.mult)
                last.then_inc(norm2, 1)

        @block.tensor
        def _(pe):
            def transpose_x(b):
                pe.wait_ge(x_loaded[b], 16)
                if b:
                    pe.wait_ge(xT_out, b)
                for t in range(TB):
                    last = pe.transpose(misc[:, t * P:(t + 1) * P], X[:, b * TB + t, :], identf[:, :])
                last.then_inc(xT_full, 1)

            pe.wait_ge(ident_ready, 1)
            transpose_x(0)
            pe.wait_ge(w_loaded, 16 * W_DMAS)
            for j in range(4):
                last = pe.transpose(slot[1][0:LORA_R, j * P:(j + 1) * P], LB[:, j, :], identf[:, :])
            last.then_inc(weights_full, 1)
            for j in range(3):
                pe.matmul(slot[2][:, j * C:(j + 1) * C], WA[:, j, :], identf[:, :], start=(j == 0), stop=False, skip_group_check=True)
            pe.wait_ge(weights_out, 1)
            pe.matmul(slot[2][:, 0:3 * C], LA[:, 0, :], lbT[:, 0:3, :].rearrange("r j p -> r (j p)"), start=False, stop=True,
                      skip_group_check=True).then_inc(weights_full, 1)
            for b in range(B):
                pe.wait_ge(xT_out, b + 1)
                if b == 0:
                    pe.wait_ge(weights_out, 2)
                for j, full, done in ((0, q_full, q_out), (1, k_full, k_out)):
                    if b:
                        pe.wait_ge(done, 2 * b)
                    pe.matmul(slot[0][:, j * T:(j + 1) * T], WT[:, j, :], xT[:, b % 2, :], start=True, stop=True).then_inc(full, 1)
                if b + 1 < B:
                    transpose_x(b + 1)
                if b:
                    pe.wait_ge(v_out, b)
                for t in range(TB):
                    last = pe.matmul(slot[1][:, T + t * C:T + (t + 1) * C], xT[:, b % 2, t * P:(t + 1) * P], WT[:, 2, :], start=True, stop=True)
                last.then_inc(v_full, 1)
                if b == 0:
                    pe.wait_ge(late_loaded, 16 * LATE_DMAS)
                    pe.matmul(slot[2][:, T:T + C], WP[:, :], identf[:, :], start=True, stop=False, skip_group_check=True)
                    pe.matmul(slot[2][:, T:T + C], LA[:, 1, :], lbT[:, 3, :], start=False, stop=True, skip_group_check=True).then_inc(weights_full, 1)

            def scores_q(g, u, n):
                qb, h0, heads = S_UNITS[u]
                v = s_view(u, n)
                per_bank = {3: 1, 2: 1, 1: 2, 0: 4}[qb]
                for h in range(0, heads, per_bank):
                    pe.matmul(v[:, h:h + per_bank, qb * P:(qb + 1) * P], identb[:, :], maskb[:, 0:per_bank, :],
                              start=True, stop=False, skip_group_check=True)
                    for j in range(h, h + per_bank):
                        head = h0 + j
                        last = pe.matmul(v[:, j, :], Qs[:, bass.ds(g, 1), head // 2, qb * P:(qb + 1) * P],
                                         Ks[:, bass.ds(g, 1), head, 0:(qb + 1) * P],
                                         start=False, stop=True, skip_group_check=True)
                last.then_inc(scores_for_max, 1)

            def scores_k(g, u, n):
                kb, h0, heads = T_UNITS[u]
                v = t_view(u, n)
                for j in range(heads):
                    head = h0 + j
                    last = pe.matmul(v[:, j, :], Ks[:, bass.ds(g, 1), head, kb * P:(kb + 1) * P],
                                     Qs[:, bass.ds(g, 1), head // 2, kb * P:T], start=True, stop=True)
                last.then_inc(scores_for_exp, 1)

            def transpose_max(g, par):
                pe.wait_ge(mparts_ready, g + 1)
                for t in range(TB):
                    last = pe.transpose(miscb[0:HQ * PARTS, t * P:(t + 1) * P],
                                        mparts[:, par, t].rearrange("p h e -> p (h e)"), identb[:, :])
                last.then_inc(mT_full, 1)

            def weighted_values(g, par, kb):
                pe.wait_ge(selected, TB * g + kb + 1)
                if kb == 0:
                    pe.wait_ge(vst_ready, g + 1)
                    pe.wait_ge(pvs_copied, g)
                for h in range(HQ):
                    last = pe.matmul(pvo[32 * h:32 * h + D + 1, kb * P:T], vst[:, par, kb, h, :], p_view(par, kb)[:, h, :],
                                     start=(kb == 0), stop=(kb == TB - 1))
                if kb == TB - 1:
                    last.then_inc(pv_done, 1)

            def transpose_pv(g):
                pe.wait_ge(pvs_copied, g + 1)
                for t in range(TB):
                    last = pe.transpose(misc[:, t * P:(t + 1) * P], pvs[:, t * P:(t + 1) * P], identf[:, :])
                last.then_inc(yT_full, 1)

            def transpose_y(b):
                pe.wait_ge(y_done, QPB * b + QPB)
                for t in range(TB):
                    last = pe.transpose(misc[:, t * P:(t + 1) * P], Y[:, t, :], identf[:, :])
                last.then_inc(fT_full, 1)

            def project(b):
                pe.wait_ge(fT_out, b + 1)
                for t in range(TB):
                    last = pe.matmul(misc[:, t * C:(t + 1) * C], yT[:, t * P:(t + 1) * P], WPT[:, :], start=True, stop=True)
                last.then_inc(proj_full, 1)

            def transpose_x1(b):
                pe.wait_ge(x1_ready, b + 1)
                for t in range(TB):
                    last = pe.transpose(misc[:, t * P:(t + 1) * P], rows[:, 0, t, 0:C], identf[:, :])
                last.then_inc(x1T_full, 1)

            def route(b):
                pe.wait_ge(x1T_out, b + 1)
                for t in range(TB):
                    last = pe.matmul(misc[:, t * E:(t + 1) * E], x1T[:, t * P:(t + 1) * P], RW[:, :], start=True, stop=True)
                last.then_inc(router_full, 1)

            def count_before(b):
                pe.wait_ge(hot_ready, b + 1)
                pe.matmul(misc[:, 0:TB * E], before[:, :], hots[:, :, :].rearrange("p t e -> p (t e)"), start=True, stop=False, skip_group_check=True)
                for t in range(TB - 1):
                    n = TB - 1 - t
                    pe.matmul(misc[:, (t + 1) * E:TB * E].rearrange("p (t e) -> p t e", e=E), onesb[:, :],
                              hots[:, t:t + 1, :].broadcast_to([P, n, E]), start=False, stop=False, skip_group_check=True)
                pe.matmul(misc[:, 0:TB * E].rearrange("p (t e) -> p t e", e=E), onesb[:, :],
                          carry[:, :].rearrange("p (a e) -> p a e", a=1).broadcast_to([P, TB, E]), start=False, stop=False, skip_group_check=True)
                pe.matmul(misc[:, TB * E:TB * E + E], onesb[:, :], carry[:, :], start=False, stop=False, skip_group_check=True)
                pe.matmul(misc[:, TB * E:TB * E + E], onesb[:, :], hot_sum[:, :], start=False, stop=True,
                          skip_group_check=True).then_inc(prefix_full, 1)

            def step(g, k, end=None, scores=True, exps=True, maxrows_=True):
                static = isinstance(g, int)
                first = static and g == 0
                par = k % 2
                last4 = end is not None
                for u in range(NU):
                    if scores:
                        if first:
                            pe.wait_ge(max_done, NU * 2)
                        if not first or u >= 2:
                            pe.wait_ge(exp_done, NU * g + u - 1)
                        scores_q(g + 2, u, (2 * u) % 3)
                    if exps:
                        if u == 0:
                            pe.wait_ge(maxrows[par], 32 * (g - par) + 64)
                        if scores:
                            pe.wait_ge(max_done, NU * g + 2 * NU + u)
                        else:
                            pe.wait_ge(max_done, NU * G)
                            pe.wait_ge(exp_done, NU * g + u - 2)
                        scores_k(g, u, (2 * u + 1) % 3)
                    if not first:
                        if u < 2:
                            weighted_values(g - 1, 1 - par, u)
                        if u == 2:
                            weighted_values(g - 1, 1 - par, 2)
                            weighted_values(g - 1, 1 - par, 3)
                    if u == 1 and maxrows_:
                        if static and g <= 1:
                            pe.wait_ge(mT_copied, g + 1)
                        else:
                            pe.wait_ge(y_done, g - 1)
                            if k == 0 and not scores:
                                pe.wait_ge(place_ready, B - 1)
                            if k == 3 and last4:
                                pe.wait_ge(stats_ready, end + 1)
                        transpose_max(g + 1, 1 - par)
                    if u == 3 and last4 and k == 3:
                        pe.wait_ge(mT_copied, g + 2)
                        transpose_x1(end)
                    if u == 4 and last4 and k == 3:
                        route(end)
                        pe.wait_ge(gap_ready, end + 1)
                        transpose_pv(g - 1)
                    if u == 3 and not first and not (last4 and k == 3):
                        if maxrows_:
                            pe.wait_ge(mT_copied, g + 2)
                        else:
                            pe.wait_ge(y_done, g - 1)
                        transpose_pv(g - 1)
                    if u == 4 and last4 and k == 2:
                        transpose_y(end)
                    if u == 5 and last4 and k == 2:
                        project(end)
                    if u == 5 and last4 and k == 3:
                        pe.wait_ge(y_done, g)
                        count_before(end)

            pe.wait_ge(consts_ready, 2)
            pe.wait_ge(stacks_loaded[0], STACK_DMAS)
            pe.wait_ge(k_out, 2 * B)
            pe.wait_ge(v_out, B)
            for g in range(2):
                for u in range(NU):
                    n = NU * g + u
                    if n >= 3:
                        pe.wait_ge(max_done, n - 2)
                    scores_q(g, u, n % 3)
                if g == 0:
                    pe.wait_ge(xT_out, B)
                    transpose_max(0, 0)
            step(0, 2)
            for b in range(1, B):
                pe.wait_ge(stacks_loaded[b], STACK_DMAS)
            step(1, 3)
            pe.wait_ge(lists_ready, 1)
            with pe.Fori(0, B - 1) as b:
                for k in range(4):
                    step(4 * b + 2 + k, k, end=b)
            step(14, 0, scores=False)
            step(15, 1, scores=False, maxrows_=False)
            for kb in range(TB):
                weighted_values(15, 1, kb)
            pe.wait_ge(y_done, 15)
            transpose_pv(15)
            transpose_y(B - 1)
            project(B - 1)
            pe.wait_ge(stats_ready, B)
            transpose_x1(B - 1)
            route(B - 1)
            pe.wait_ge(gap_ready, B)
            count_before(B - 1)

            def transpose_rows(j, ring):
                if isinstance(j, int):
                    pe.wait_ge(xg_loaded[ring], 16 * (j // RING + 1))
                else:
                    pe.wait_ge(xg_loaded[ring], 16 * ((j - ring) // RING + 1))
                pe.transpose(misc[:, 0:P], xg[:, ring, 0:C], identf[:, :]).then_inc(xgT_full, 1)

            def gate_up(s, two):
                e = pe.value_load(expert_of[0:1, bass.ds(s, 1)], min_val=0, max_val=E - 1)
                pe.wait_ge(xgT_ready, s + 1)
                if not isinstance(s, int) or s >= 2:
                    pe.wait_ge(h_ready, s - 1)
                for w in range(2):
                    last = pe.matmul(slot[two][:, w * T:w * T + F], xgT[:, two, :],
                                     GUW[:, bass.ds(e, 1), w, :].rearrange("p e f -> p (e f)"), start=True, stop=True)
                last.then_inc(gu_full, 1)

            def transpose_hidden(j, two):
                pe.wait_ge(h_ready, j + 1)
                for k, (f0, fn) in enumerate(FC):
                    last = pe.transpose(slot[2][0:fn, two * T + k * P:two * T + (k + 1) * P], hid[:, two, f0:f0 + fn], identf[:, :])
                last.then_inc(hT_full, 1)

            def down(j, two):
                e = pe.value_load(expert_of[0:1, bass.ds(j, 1)], min_val=0, max_val=E - 1)
                pe.wait_ge(hT_ready, j + 1)
                if not isinstance(j, int) or j >= 1:
                    pe.wait_ge(ys_ready, j)
                for k, (f0, fn) in enumerate(FC):
                    last = pe.matmul(pvo[:, 0:C], hT[0:fn, two, k, :], DW[0:fn, bass.ds(e, 1), k, :].rearrange("p e c -> p (e c)"),
                                     start=(k == 0), stop=(k == NFC - 1))
                last.then_inc(y_full, 1)

            def expert_step(s, m):
                static = isinstance(s, int)
                if not static or s < ET:
                    gate_up(s, m % 2)
                if not static or 1 <= s <= ET:
                    transpose_hidden(s - 1, (m - 1) % 2)
                if not static or s + 1 < ET:
                    transpose_rows(s + 1, (m + 1) % RING)
                if not static or s >= 2:
                    down(s - 2, m % 2)

            pe.wait_ge(tables_ready, 1)
            pe.wait_ge(experts_loaded, 16 * (2 + NFC))
            pe.wait_ge(exp_done, NU * G)
            pe.wait_ge(place_ready, B)
            transpose_rows(0, 0)
            expert_steps(pe, expert_step)


_INS = ['L0_attn_x', 'L0_attn_w_attn', 'L0_attn_b_attn', 'L0_attn_la_attn', 'L0_attn_lb_attn', 'L0_attn_w_proj',
        'L0_attn_b_proj', 'L0_attn_la_proj', 'L0_attn_lb_proj', 'L0_ffn_router_w', 'L0_ffn_gate_proj',
        'L0_ffn_up_proj', 'L0_ffn_down_proj']
_OUTS = [((4, 512, 128), 'float32')]


def kernel(**inputs):
    import numpy as _np
    import concourse.bacc as _bacc
    from concourse import mybir as _mybir
    from concourse.bass_utils import run_bass_kernel_spmd as _run

    nc = _bacc.Bacc("TRN2", target_bir_lowering=False, num_devices=1)
    arrays, args = {}, []
    for name in _INS:
        a = _np.ascontiguousarray(inputs[name])
        arrays[f"in_{name}_dram"] = a
        args.append(nc.dram_tensor(f"in_{name}_dram", a.shape, _mybir.dt.from_np(a.dtype), kind="ExternalInput").ap())
    for i, (shape, dtype) in enumerate(_OUTS):
        dt = _mybir.dt.from_np(_np.dtype(dtype))
        args.append(nc.dram_tensor(f"out_{i}_dram", shape, dt, kind="ExternalOutput").ap())
    args.append(nc.dram_tensor("parts_scratch", (4, 2, 128, 6 * 512), _mybir.dt.bfloat16).ap())
    args.append(nc.dram_tensor("rows_scratch", (8 * (2048 + 256), 130), _mybir.dt.float32).ap())
    args.append(nc.dram_tensor("chosen_scratch", (2 * 2048, 128), _mybir.dt.float32).ap())
    causal_attention_then_top2_experts(nc, *args)
    r = _run(nc, [arrays], core_ids=[0])
    return r.results[0]["out_0_dram"]
```

```python
from contextlib import ExitStack

import concourse.bass as bass
from concourse import mybir

ALU = mybir.AluOpType
ACT = mybir.ActivationFunctionType
F32 = mybir.dt.float32
BF16 = mybir.dt.bfloat16
I32 = mybir.dt.int32
U32 = mybir.dt.uint32
AX_X = mybir.AxisListType.X

P = 128


def causal_attention_then_top2_experts(
    nc: bass.Bass,
    x: bass.AP, w_attn: bass.AP, b_attn: bass.AP, la_attn: bass.AP, lb_attn: bass.AP,
    w_proj: bass.AP, b_proj: bass.AP, la_proj: bass.AP, lb_proj: bass.AP,
    router_w: bass.AP, gate_proj: bass.AP, up_proj: bass.AP, down_proj: bass.AP,
    out: bass.AP, parts_scratch: bass.AP, rows_scratch: bass.AP, chosen_scratch: bass.AP,
):
    B, T, C = x.shape
    H = 16
    D = C // H
    LORA_R = la_attn.shape[0]
    LORA_SCALE = 0.5
    SCALE = float(D) ** -0.5
    EPS = 1e-5
    NEG = -3.0e38
    E = router_w.shape[1]
    F = gate_proj.shape[2]
    TOKENS = B * T
    NT = TOKENS // P
    TB = T // P
    HQ = 4
    QPB = H // HQ
    G = B * QPB
    PARTS = 3
    PRODUCTS = 6
    Q_SLOTS = ((0, 3, 0), (3, 2, 1), (5, 1, 2))
    K_SLOTS = ((0, 3, None), (3, 2, None), (5, 1, None))
    HALF = P // 2
    FC = [(c, min(P, F - c)) for c in range(0, F, P)]
    NFC = len(FC)
    REGION = TOKENS + 2 * P
    MAX_TILES = TOKENS // P
    ET = (2 * TOKENS + E * (P - 1)) // P
    ROW = C + 2
    NO_ROW = 1 << 20
    ONE_ONE = 0x3F803F80
    RING = 8
    OUT_RING = 4
    POOL_ADDS = (1, 2, 3)
    assert (T, C, TB, QPB) == (512, P, 4, 4) and PARTS + D * PRODUCTS <= HALF

    x_tiles = x.rearrange("b (t p) c -> p (b t) c", p=P)
    out_tiles = out.rearrange("b (t p) c -> p (b t) c", p=P)
    chosen = chosen_scratch.rearrange("(j t p) c -> j p t c", j=2, p=P)

    with ExitStack() as ctx:
        def sb(name, shape, dt=F32):
            return ctx.enter_context(nc.sbuf_tensor(name, shape, dt))

        def pb(name, shape, dt=F32):
            return ctx.enter_context(nc.psum_tensor(name, shape, dt))

        def sem(name):
            return ctx.enter_context(nc.semaphore(name))

        X = sb("X", [P, NT, C])
        WA = sb("WA", [P, 3, C])
        WP = sb("WP", [P, C])
        LB = sb("LB", [P, 4, LORA_R])
        LA = sb("LA", [LORA_R, 2, C])
        lbT = sb("lbT", [LORA_R, 4, P])
        WT = sb("WT", [P, 3, C])
        WPT = sb("WPT", [P, C])
        RW = sb("RW", [P, E])
        bqk = sb("bqk", [P, 2])
        bv_rows = sb("bv_rows", [P, C])
        bp_rows = sb("bp_rows", [P, C])
        identf = sb("identf", [P, P])
        identb = sb("identb", [P, P], BF16)
        before = sb("before", [P, P], BF16)
        onesb = sb("onesb", [P, P], BF16)
        maskb = sb("maskb", [P, HQ, P], BF16)
        mask_after = sb("mask_after", [P, HQ, P], BF16)
        blank_k = sb("blank_k", [P, 2, T], BF16)
        blank_q = sb("blank_q", [P, T], BF16)
        PW = [(TB - kb) * P for kb in range(TB)]
        POFF = [HQ * sum(PW[:kb]) for kb in range(TB)]
        Pt = sb("Pt", [P, 2, HQ * sum(PW)])
        free_p = Pt[:, :, :].rearrange("p n t -> p (n t)")
        xT = free_p[:, 0:2 * T].rearrange("p (n t) -> p n t", n=2)
        qk = free_p[:, 2 * T:4 * T].rearrange("p (s t) -> p s t", s=2)
        rest = free_p[:, 4 * T:6 * T].rearrange("p (s t) -> p s t", s=2)
        early_parts = free_p[:, 6 * T:6 * T + 2 * PARTS * T].bitcast(BF16).rearrange("p (b s e t) -> p b s e t", b=2, s=2, e=PARTS)
        EARLY = 8 * T
        early = sb("early", [P, EARLY])
        late_parts = early[:, 0:2 * PARTS * T].bitcast(BF16).rearrange("p (b s e t) -> p b s e t", b=2, s=2, e=PARTS)
        parts = [early_parts[:, 0], early_parts[:, 1], late_parts[:, 0], late_parts[:, 1]]
        early_taken = [0]

        def reuse(*shape):
            n = 1
            for extent in shape:
                n *= extent
            flat = early[:, early_taken[0]:early_taken[0] + n]
            early_taken[0] += n
            assert early_taken[0] <= EARLY
            names = "abcd"[:len(shape)]
            return flat.rearrange(f"p ({' '.join(names)}) -> p {' '.join(names)}",
                                  **{name: extent for name, extent in zip(names[1:], shape[1:])})

        Qs = sb("Qs", [P, G, 2, T], BF16)
        Ks = sb("Ks", [P, G, HQ, T], BF16)
        V9 = sb("V9", [P, G, TB, HQ, D + 1])
        vst = sb("vst", [P, 2, TB, HQ, D + 1])
        negm = sb("negm", [P, 2, TB, HQ])
        mrest = sb("mrest", [P, 2, TB, HQ])
        mparts = sb("mparts", [P, 2, TB, HQ, PARTS], BF16)
        mT = sb("mT", [HQ * PARTS, 2, T], BF16)
        pvs = sb("pvs", [P, T])
        rl = sb("rl", [P, TB, HQ])
        Y = reuse(TB, C)
        yT = reuse(T)
        XR = reuse(TB, C)
        stats = sb("stats", [P, TB, 6])
        mv2 = sb("mv2", [P, B, TB, 2])
        veps2 = sb("veps2", [P, B, TB])
        rstd2 = sb("rstd2", [P, B, TB])
        shift2 = sb("shift2", [P, B, TB])
        mv = sb("mv", [P, TB, 2])
        veps = sb("veps", [P, TB])
        rstd = sb("rstd", [P, TB])
        minus_half = sb("minus_half", [P, TB])
        x1T = reuse(T)
        rows = reuse(2, TB, ROW)
        numbers = sb("numbers", [P, 2, NT], I32)
        lanes = sb("lanes", [P, TB, E])
        sc = sb("sc", [P, TB, E])
        top = sb("top", [P, TB, 8])
        topi = sb("topi", [P, TB, 8], U32)
        topf = sb("topf", [P, 2, TB])
        hot = sb("hot", [P, 2, TB, E])
        hots = sb("hots", [P, TB, E], BF16)
        hot_sum = sb("hot_sum", [P, E], BF16)
        carry = sb("carry", [P, E], BF16)
        ranks = sb("ranks", [P, 2, TB, E])
        rank = sb("rank", [P, 2, TB])
        place = sb("place", [P, 2, TB], U32)
        gap = sb("gap", [P, TB])
        egap = sb("egap", [P, TB])
        steps16 = sb("steps16", [P, E, MAX_TILES])
        over = reuse(E, MAX_TILES)
        count = sb("count", [P, E])
        ntiles = sb("ntiles", [P, E])
        lower = sb("lower", [P, E, E])
        prod8 = reuse(E, E)
        ends = sb("ends", [P, E])
        tile_no = sb("tile_no", [P, ET, E])
        past = reuse(ET, E)
        pastn = reuse(ET, E)
        expert_f = sb("expert_f", [P, ET])
        first_f = sb("first_f", [P, ET])
        behind = sb("behind", [P, ET])
        expert_of = sb("expert_of", [P, ET], I32)
        row_of = sb("row_of", [P, ET], I32)
        fill_f = sb("fill_f", [P, E])
        fill_row = sb("fill_row", [P, E], I32)
        region_f = sb("region_f", [P, E])
        fill = sb("fill", [P, 2, ROW])
        free_k = Ks[:, :, :, :].rearrange("p g h t -> p (g h t)").bitcast(F32)
        GUW = free_k[:, 0:2 * E * F].rearrange("p (e w f) -> p e w f", e=E, w=2)
        DW = free_k[:, 2 * E * F:2 * E * F + E * NFC * C].rearrange("p (e k c) -> p e k c", e=E, k=NFC)
        taken = [0]

        def take(n):
            taken[0] += n
            return free_p[:, taken[0] - n:taken[0]]

        xg = take(RING * ROW).rearrange("p (n c) -> p n c", n=RING)
        xgT = take(2 * P).rearrange("p (n t) -> p n t", n=2)
        sg = take(2 * F).rearrange("p (n f) -> p n f", n=2)
        hid = take(2 * F).rearrange("p (n f) -> p n f", n=2)
        hT = take(2 * NFC * P).rearrange("p (n k t) -> p n k t", n=2, k=NFC)
        ys = take(OUT_RING * C).rearrange("p (n c) -> p n c", n=OUT_RING)
        back = Qs[:, :, :, :].rearrange("p g c t -> p (g c t)").bitcast(F32)[:, 0:2 * B * TB * C].rearrange("p (b j t c) -> p b j t c", b=B, j=2, t=TB)

        slot = [pb(f"slot{i}", [P, 2 * T]) for i in range(3)]
        pvo = pb("pvo", [P, T])
        misc = pb("misc", [P, T])
        miscb = misc[:, :].bitcast(BF16)

        lb_loaded, w_loaded, late_loaded = sem("lb_loaded"), sem("w_loaded"), sem("late_loaded")
        x_loaded = [sem(f"x_loaded{b}") for b in range(B)]
        consts_ready, ident_ready, ident0, mask_ready = sem("consts_ready"), sem("ident_ready"), sem("ident0"), sem("mask_ready")
        blanks_ready, blanked = sem("blanks_ready"), [sem(f"blanked{b}") for b in range(B)]
        zeroed = sem("zeroed")
        weights_full, weights_out = sem("weights_full"), sem("weights_out")
        xT_full, xT_out = sem("xT_full"), sem("xT_out")
        q_full, k_full, v_full = sem("q_full"), sem("k_full"), sem("v_full")
        q_out, k_out, v_out = sem("q_out"), sem("k_out"), sem("v_out")
        qsplit, ksplit, split_chain = sem("qsplit"), sem("ksplit"), sem("split_chain")
        parts_stored = [[sem(f"parts_stored{s}{b}") for b in range(B)] for s in range(2)]
        stacks_loaded = sem("stacks_loaded")
        scores_for_max, max_done = sem("scores_for_max"), sem("max_done")
        scores_for_exp, exp_done = sem("scores_for_exp"), sem("exp_done")
        mchain, mparts_ready = sem("mchain"), sem("mparts_ready")
        mT_full, mT_copied = sem("mT_full"), sem("mT_copied")
        maxrows = [sem("maxrows0"), sem("maxrows1")]
        selected, vst_ready = sem("selected"), sem("vst_ready")
        pv_done, pvs_copied = sem("pv_done"), sem("pvs_copied")
        yT_full, rl_ready, y_done = sem("yT_full"), sem("rl_ready"), sem("y_done")
        pool_passed, dve_passed = sem("pool_passed"), sem("dve_passed")
        xb_ready, lists_ready = sem("xb_ready"), sem("lists_ready")
        fT_full, fT_out, proj_full = sem("fT_full"), sem("fT_out"), sem("proj_full")
        dchain = sem("dchain")
        stats_ready, veps_ready, rstd_ready = sem("stats_ready"), sem("veps_ready"), sem("rstd_ready")
        x1_ready, x1T_full, x1T_out = sem("x1_ready"), sem("x1T_full"), sem("x1T_out")
        router_full, scores_copied, hot_ready, gap_ready, egap_ready = sem("router_full"), sem("scores_copied"), sem("hot_ready"), sem("gap_ready"), sem("egap_ready")
        prefix_full, place_ready, numbered, scattered = sem("prefix_full"), sem("place_ready"), sem("numbered"), sem("scattered")
        fills_ready, tables_ready, filled = sem("fills_ready"), sem("tables_ready"), sem("filled")
        experts_loaded = sem("experts_loaded")
        xg_loaded = [sem(f"xg_loaded{i}") for i in range(RING)]
        xgT_full, xgT_ready = sem("xgT_full"), sem("xgT_ready")
        gate_full, gu_full, silu_done, h_ready = sem("gate_full"), sem("gu_full"), sem("silu_done"), sem("h_ready")
        hT_full, hT_ready, y_full, ys_ready = sem("hT_full"), sem("hT_ready"), sem("y_full"), sem("ys_ready")
        y_scattered = [sem(f"y_scattered{i}") for i in range(RING)]
        back_loaded = [sem(f"back_loaded{i}") for i in range(B)]
        first_added, shift_ready, norm2, last_half, out_stored = sem("first_added"), sem("shift_ready"), sem("norm2"), sem("last_half"), sem("out_stored")

        S_UNITS = [(3, 0, 2), (3, 2, 2), (2, 0, 2), (2, 2, 2), (1, 0, 4), (0, 0, 4)]
        T_UNITS = [(0, 0, 2), (0, 2, 2), (1, 0, 2), (1, 2, 2), (2, 0, 4), (3, 0, 4)]
        NU = len(S_UNITS)
        MASKED_FROM = G - 2
        PV_AT = ((0, 1, 2), (0, 1, 1))

        def s_view(u, n):
            qb, _, heads = S_UNITS[u]
            return slot[n][:, :].rearrange("p (h k) -> p h k", k=[128, 256, 512, 512][qb])[:, 0:heads, 0:(qb + 1) * P]

        def t_view(u, n):
            kb, _, heads = T_UNITS[u]
            return slot[n][:, :].rearrange("p (h k) -> p h k", k=[512, 512, 256, 128][kb])[:, 0:heads, 0:PW[kb]]

        def p_view(par, kb):
            return Pt[:, par, POFF[kb]:POFF[kb] + HQ * PW[kb]].rearrange("p (h q) -> p h q", h=HQ)

        def number_column(j):
            return rows[:, j, :, C:C + 1].rearrange("p t a -> p (t a)").bitcast(I32)

        W_DMAS = 3
        LATE_DMAS = 4
        STACK_DMAS = 2 * 2 * 16
        LOOP_FROM = 8
        LOOP_ENDS = LOOP_FROM + (ET - 1 - LOOP_FROM) // RING * RING

        def expert_steps(eng, step):
            for s in range(LOOP_FROM):
                step(s, s % RING)
            with eng.Fori(0, (LOOP_ENDS - LOOP_FROM) // RING) as i:
                for r in range(RING):
                    step(RING * i + (LOOP_FROM + r), (LOOP_FROM + r) % RING)
            for s in range(LOOP_ENDS, ET + 2):
                step(s, s % RING)

        block = ctx.enter_context(nc.Block())

        @block.sync
        def _(sp):
            sp.dma_start(X[:, 0:TB, :], x_tiles[:, 0:TB, :]).then_inc(x_loaded[0], 16)
            sp.dma_start(LB[:, 0:3, :], lb_attn.rearrange("(j p) r -> p j r", p=P)).then_inc(lb_loaded, 16)
            sp.dma_start(LB[:, 3, :], lb_proj).then_inc(lb_loaded, 16)
            sp.dma_start(WA[:, :, :], w_attn.rearrange("(j p) c -> p j c", p=P)).then_inc(w_loaded, 16)
            sp.dma_start(LA[:, 0, :], la_attn).then_inc(w_loaded, 16)
            sp.dma_start(bqk[:, :], b_attn[0:2 * C].rearrange("(j p) -> p j", p=P), allow_slow_non_contiguous=True).then_inc(w_loaded, 16)
            for b in range(1, B):
                sp.dma_start(X[:, b * TB:(b + 1) * TB, :], x_tiles[:, b * TB:(b + 1) * TB, :]).then_inc(x_loaded[b], 16)

            def store_parts(b):
                for s, split, slots in ((0, qsplit, Q_SLOTS), (1, ksplit, K_SLOTS)):
                    sp.wait_ge(split, b + 1)
                    dst = parts_scratch[b, s].rearrange("(p e) t -> p e t", e=PRODUCTS)
                    for first, n, part in slots:
                        src = parts[b][:, s, 0:n, :] if part is None else parts[b][:, s, part:part + 1, :].broadcast_to([P, n, T])
                        sp.dma_start(dst[:, first:first + n, :], src).then_inc(parts_stored[s][b], 16)

            def load_stacks(b):
                if b:
                    sp.wait_ge(stacks_loaded, STACK_DMAS * b)
                sp.wait_ge(blanked[b], 1)
                for s in range(2):
                    sp.wait_ge(parts_stored[s][b], 16 * PARTS)
                    src = parts_scratch[b, s].rearrange("(j a r) t -> a r j t", a=2, r=D * PRODUCTS)
                    for a in range(2):
                        row = HALF * a + PARTS
                        if s == 0:
                            dst = Qs[row:row + D * PRODUCTS, QPB * b:QPB * (b + 1)].rearrange("p g c t -> p (g c) t")
                        else:
                            dst = Ks[row:row + D * PRODUCTS, QPB * b:QPB * (b + 1)].rearrange("p g (c a) t -> p a (g c) t", a=2)[:, a]
                        sp.dma_start(dst, src[a]).then_inc(stacks_loaded, 16)

            def store_maxrows(g, par):
                sp.wait_ge(mT_copied, g + 1)
                for h in range(HQ):
                    sp.dma_start(Qs[HALF * (h % 2):HALF * (h % 2) + PARTS, bass.ds(g, 1), h // 2, :],
                                 mT[PARTS * h:PARTS * (h + 1), par, :]).then_inc(maxrows[par], 16)

            for b in range(2):
                store_parts(b)
                load_stacks(b)
            store_maxrows(0, 0)
            for b in range(2, B):
                store_parts(b)
            store_maxrows(1, 1)
            load_stacks(2)
            store_maxrows(2, 0)
            store_maxrows(3, 1)
            load_stacks(3)
            with sp.Fori(2, G // 2) as pair:
                store_maxrows(2 * pair, 0)
                store_maxrows(2 * pair + 1, 1)
            sp.wait_ge(scores_for_exp, NU * G)
            for w, src in enumerate((gate_proj, up_proj)):
                sp.dma_start(GUW[:, :, w, :], src.rearrange("e d f -> d e f")).then_inc(experts_loaded, 16)
            for k, (f0, fn) in enumerate(FC):
                sp.dma_start(DW[0:fn, :, k, :], down_proj[:, f0:f0 + fn, :].rearrange("e f c -> f e c")).then_inc(experts_loaded, 16)
            sp.wait_ge(fills_ready, 1)
            for e in range(0, E, 2):
                at = sp.value_load(fill_row[0:1, e:e + 1], min_val=e * REGION, max_val=e * REGION + TOKENS)
                sp.dma_start(rows_scratch[bass.ds(at, 2 * P), :].rearrange("(p a) c -> p (a c)", a=2),
                             fill[:, :, :].rearrange("p a c -> p (a c)")).then_inc(filled, 16)
            sp.wait_ge(tables_ready, 1)

            def first_row(j):
                return sp.value_load(row_of[0:1, bass.ds(j, 1)], min_val=0, max_val=E * REGION - P)

            def load_rows(j, ring, at=None):
                if at is None:
                    at = first_row(j)
                sp.dma_start(xg[:, ring, :], rows_scratch[bass.ds(at, P), :]).then_inc(xg_loaded[ring], 16)

            first_rows = [first_row(j) for j in range(4)]
            sp.wait_ge(scattered, 16 + 2 * TB * B * 16)
            sp.wait_ge(filled, 16 * E)
            sp.wait_ge(pv_done, G)
            for j in range(RING):
                load_rows(j, j, first_rows[j] if j < len(first_rows) else None)
            with sp.Fori(1, ET // RING) as i:
                for r in range(RING):
                    sp.wait_ge(y_scattered[r], 16 * i)
                    load_rows(RING * i + r, r)
            for j in range(ET // RING * RING, ET):
                sp.wait_ge(y_scattered[j % RING], 16 * (j // RING))
                load_rows(j, j % RING)
            for r in range(RING):
                sp.wait_ge(y_scattered[r], 16 * len(range(r, ET, RING)))
            for b in range(B):
                for j in range(2):
                    sp.dma_start(back[:, b, j], chosen[j, :, b * TB:(b + 1) * TB, :]).then_inc(back_loaded[b], 16)
            for b in range(B):
                sp.wait_ge(norm2, b + 1)
                if b == B - 1:
                    sp.wait_ge(last_half, 1)
                sp.dma_start(out_tiles[:, b * TB:(b + 1) * TB, :], X[:, b * TB:(b + 1) * TB, :]).then_inc(out_stored, 16)
            sp.wait_ge(out_stored, 16 * B)

        @block.gpsimd
        def _(pool):
            pool.dma_start(RW[:, :], router_w).then_inc(scattered, 16)
            pool.memset(identf[:, :], 0.0).then_inc(ident0, 1)
            pool.memset(maskb[:, :, :], 0.0).then_inc(ident0, 1)
            pool.wait_ge(ident0, 2)
            pool.affine_select(out=identf[:, :], in_=identf[:, :], compare_op=ALU.not_equal, fill=1.0,
                               base=0, pattern=[[-1, P]], channel_multiplier=1).then_inc(ident_ready, 1)
            pool.affine_select(out=maskb[:, :, :], in_=maskb[:, :, :], compare_op=ALU.is_ge, fill=NEG,
                               base=0, pattern=[[0, HQ], [-1, P]], channel_multiplier=1).then_inc(consts_ready, 1)
            pool.wait_ge(ident_ready, 1)
            pool.tensor_copy(identb[:, :], identf[:, :]).then_inc(consts_ready, 1)
            pool.memset(carry[:, :], 0.0)
            pool.memset(minus_half[:, :], -0.5)
            pool.memset(onesb[:, :], 1.0).then_inc(ident0, 1)
            pool.wait_ge(ident0, 3)
            pool.affine_select(out=before[:, :], in_=onesb[:, :], compare_op=ALU.is_gt, fill=0.0,
                               base=0, pattern=[[1, P]], channel_multiplier=-1)
            pool.memset(mask_after[:, :, :], 0.0).then_inc(ident0, 1)
            pool.wait_ge(ident0, 4)
            pool.affine_select(out=mask_after[:, :, :], in_=mask_after[:, :, :], compare_op=ALU.is_ge, fill=NEG,
                               base=0, pattern=[[0, HQ], [1, P]], channel_multiplier=-1).then_inc(mask_ready, 1)
            for i, b in enumerate(range(2, B)):
                quads = slice(QPB * b, QPB * (b + 1))
                pool.memset(Ks[:, quads].rearrange("p g h t -> p (g h t)").bitcast(I32), 0).then_inc(zeroed, 1)
                pool.memset(Qs[:, quads].rearrange("p g c t -> p (g c t)").bitcast(I32), 0).then_inc(zeroed, 1)
                pool.wait_ge(zeroed, 2 * i + 2)
                for a in range(2):
                    heads = Ks[HALF * a:HALF * a + PARTS, quads].rearrange("p g (c a) t -> p a (g c) t", a=2)[:, a]
                    last = pool.memset(heads.bitcast(I32), ONE_ONE)
                last.then_inc(blanked[b], 1)
                pool.wait_ge(blanked[b], 1)
            pool.iota(lanes[:, :, :], pattern=[[0, TB], [1, E]], base=0, channel_multiplier=0,
                      allow_small_or_imprecise_dtypes=True)
            pool.iota(numbers[:, :, :], pattern=[[TOKENS, 2], [P, NT]], base=0, channel_multiplier=1)
            pool.iota(steps16[:, :, :], pattern=[[0, E], [P, MAX_TILES]], base=0, channel_multiplier=0,
                      allow_small_or_imprecise_dtypes=True)
            pool.iota(tile_no[:, :, :], pattern=[[1, ET], [0, E]], base=0, channel_multiplier=0,
                      allow_small_or_imprecise_dtypes=True)
            pool.iota(region_f[:, :], pattern=[[REGION, E]], base=0, channel_multiplier=0,
                      allow_small_or_imprecise_dtypes=True)
            pool.memset(lower[:, :, :], 1.0).then_inc(ident0, 1)
            pool.wait_ge(ident0, 5)
            pool.affine_select(out=lower[:, :, :], in_=lower[:, :, :], compare_op=ALU.is_ge, fill=0.0,
                               base=0, pattern=[[1, E], [-1, E]], channel_multiplier=0)
            pool.memset(fill[:, :, :], 0.0).then_inc(ident0, 1)
            pool.wait_ge(ident0, 6)
            pool.memset(fill[:, :, C:C + 1].bitcast(I32), NO_ROW).then_inc(lists_ready, 1)
            pool.wait_ge(xT_full, B)
            pool.wait_ge(late_loaded, 16 * LATE_DMAS)
            for t in range(NT):
                last = pool.tensor_tensor(X[:, t, :], X[:, t, :], bp_rows[:, :], ALU.add)
            last.then_inc(xb_ready, 1)

            def wait_counted(semaphore, count_):
                pool.wait_ge(semaphore, count_)
                pool.sem_inc(pool_passed, 1)

            def split_max(g, par):
                wait_counted(max_done, NU * g + NU)
                if not isinstance(g, int) or g >= 2:
                    wait_counted(mT_full, g - 1)
                m = negm[:, par]
                r = mrest[:, par]
                p = [mparts[:, par, :, :, e] for e in range(PARTS)]
                pool.tensor_copy(p[0], m).then_inc(mchain, 1)
                pool.wait_ge(mchain, 3 * g + 1)
                pool.tensor_tensor(r, m, p[0], ALU.subtract).then_inc(mchain, 1)
                wait_counted(mchain, 3 * g + 2)
                pool.tensor_copy(p[1], r).then_inc(mchain, 1)
                pool.wait_ge(mchain, 3 * g + 3)
                pool.tensor_tensor(p[2], r, p[1], ALU.subtract).then_inc(mparts_ready, 1)

            def select(g, par, kb):
                wait_counted(exp_done, NU * g + [2, 4, 5, 6][kb])
                v = p_view(par, kb)[:, :, 0:P]
                pool.affine_select(out=v, in_=v, compare_op=ALU.is_ge, fill=0.0, base=0,
                                   pattern=[[0, HQ], [1, P]], channel_multiplier=-1).then_inc(selected, 1)

            def inverse_deviation(b):
                wait_counted(stats_ready, b + 1)
                pool.tensor_scalar(veps[:, :], mv[:, :, 1], EPS, None, ALU.add).then_inc(veps_ready, 1)
                pool.wait_ge(veps_ready, b + 1)
                pool.tensor_tensor(rstd[:, :], veps[:, :], minus_half[:, :], ALU.pow).then_inc(rstd_ready, 1)

            def number_rows(b):
                wait_counted(scattered, 16 + 2 * TB * 16 * b)
                for j in range(2):
                    pool.tensor_copy(number_column(j), numbers[:, j, bass.ds(b * TB, TB)])
                wait_counted(x1_ready, b + 1)
                pool.tensor_copy(rows[:, 1, :, 0:C], rows[:, 0, :, 0:C])
                pool.tensor_copy(X[:, bass.ds(b * TB, TB), :], rows[:, 0, :, 0:C]).then_inc(numbered, 1)

            def scatter_rows(b, j, t):
                if j == 0 and t == 0:
                    wait_counted(place_ready, b + 1)
                    wait_counted(numbered, b + 1)
                pool.indirect_dma_start(rows_scratch, bass.IndirectOffsetOnAxis(place[:, j, t:t + 1], 0),
                                        rows[:, j, t, :], None).then_inc(scattered, 16)

            def step(g, k, end=None, chosen_before=None, scores=True):
                selects = not isinstance(g, int) or g < MASKED_FROM
                par = k % 2
                if end is not None:
                    inverse_deviation(end)
                if not isinstance(g, int) or g >= 2:
                    wait_counted(pv_done, g - 1)
                pool.tensor_copy(vst[:, par].rearrange("p t h d -> p (t h d)"),
                                 V9[:, bass.ds(g, 1)].rearrange("p g t h d -> p (g t h d)")).then_inc(vst_ready, 1)
                for kb in range(TB):
                    if selects:
                        select(g, par, kb)
                    if kb == 1 and end is not None:
                        number_rows(end)
                    if kb == TB - 1 and scores:
                        split_max(g + 2, par)
                    if chosen_before is not None:
                        scatter_rows(chosen_before, k, kb)

            split_max(0, 0)
            split_max(1, 1)
            pool.wait_ge(v_out, B)
            step(0, 2)
            step(1, 3)
            step(2, 0)
            step(3, 1)
            with pool.Fori(0, B - 2) as b:
                step(4 * b + 4, 2)
                step(4 * b + 5, 3, end=b)
                step(4 * b + 6, 0, chosen_before=b)
                step(4 * b + 7, 1, chosen_before=b)
            step(G - 4, 2)
            step(G - 3, 3, end=B - 2)
            step(G - 2, 0, chosen_before=B - 2, scores=False)
            step(G - 1, 1, chosen_before=B - 2, scores=False)
            inverse_deviation(B - 1)
            number_rows(B - 1)
            for j in range(2):
                for t in range(TB):
                    scatter_rows(B - 1, j, t)

            def scatter_results(j, ring):
                wait_counted(ys_ready, j + 1)
                pool.indirect_dma_start(chosen_scratch, bass.IndirectOffsetOnAxis(xg[:, ring, C:C + 1].bitcast(U32), 0),
                                        ys[:, ring % OUT_RING, :], None, bounds_check=2 * TOKENS - 1,
                                        oob_is_err=False).then_inc(y_scattered[ring], 16)

            with pool.Fori(0, ET // RING) as i:
                for r in range(RING):
                    scatter_results(RING * i + r, r)
            for j in range(ET // RING * RING, ET):
                scatter_results(j, j % RING)

            def last_deviation(b):
                pool.wait_ge(stats_ready, B + b + 1)
                pool.tensor_scalar(veps2[:, b], mv2[:, b, :, 1], EPS, None, ALU.add).then_inc(veps_ready, 1)
                pool.wait_ge(veps_ready, B + b + 1)
                pool.tensor_tensor(rstd2[:, b], veps2[:, b], minus_half[:, :], ALU.pow).then_inc(rstd_ready, 1)

            for b in POOL_ADDS:
                pool.wait_ge(back_loaded[b], 32)
                xb = X[:, b * TB:(b + 1) * TB, :].rearrange("p t c -> p (t c)")
                pool.tensor_tensor(xb, xb, back[:, b, 0].rearrange("p t c -> p (t c)"), ALU.add).then_inc(first_added, 1)
                last_deviation(b - 1)
            for b in range(max(POOL_ADDS), B):
                last_deviation(b)

        @block.scalar
        def _(act):
            for dst, src in ((LA[:, 1, :], la_proj), (WP[:, :], w_proj),
                             (bv_rows[:, :], b_attn[2 * C:3 * C].rearrange("(a c) -> a c", a=1).broadcast_to([P, C])),
                             (bp_rows[:, :], b_proj.rearrange("(a c) -> a c", a=1).broadcast_to([P, C]))):
                act.dma_start(dst, src).then_inc(late_loaded, 16)
            for b in range(B):
                act.wait_ge(xT_full, b + 1)
                if b >= 2:
                    act.wait_ge(v_full, b - 1)
                act.activation(xT[:, b % 2, :], misc[:, :], ACT.Copy).then_inc(xT_out, 1)
                for s, full, split, done in ((0, q_full, qsplit, q_out), (1, k_full, ksplit, k_out)):
                    act.wait_ge(full, b + 1)
                    if b == 0:
                        act.wait_ge(w_loaded, 16 * W_DMAS)
                    else:
                        act.wait_ge(split, b)
                    src = slot[2 * (b % 2)][:, s * T:(s + 1) * T]
                    act.activation(parts[b][:, s, 0, :], src, ACT.Identity, bias=bqk[:, s:s + 1]).then_inc(done, 1)
                    act.activation(qk[:, s, :], src, ACT.Identity, bias=bqk[:, s:s + 1]).then_inc(done, 1)

            def copy_mT(g, par):
                act.wait_ge(mT_full, g + 1)
                act.activation(mT[:, par, :], miscb[0:HQ * PARTS, 0:T], ACT.Copy).then_inc(mT_copied, 1)

            def copy_pv(g):
                act.wait_ge(pv_done, g + 1)
                if not isinstance(g, int) or g >= 1:
                    act.wait_ge(yT_full, g)
                act.activation(pvs[:, :], pvo[:, :], ACT.Copy).then_inc(pvs_copied, 1)

            def copy_yT(b):
                act.wait_ge(fT_full, b + 1)
                act.activation(yT[:, :], misc[:, :], ACT.Copy).then_inc(fT_out, 1)

            def copy_x1(b):
                act.wait_ge(x1T_full, b + 1)
                act.activation(x1T[:, :], misc[:, :], ACT.Copy).then_inc(x1T_out, 1)

            def copy_scores(b):
                act.wait_ge(router_full, b + 1)
                act.activation(sc[:, :, :].rearrange("p t e -> p (t e)"), misc[:, 0:TB * E], ACT.Copy).then_inc(scores_copied, 1)

            def exp_gap(b):
                act.wait_ge(gap_ready, b + 1)
                act.activation(egap[:, :], gap[:, :], ACT.Exp).then_inc(egap_ready, 1)

            def step(g, k, end=None, pv=True, maxrows=True):
                par = k % 2
                for u in range(NU):
                    kb, h0, heads = T_UNITS[u]
                    act.wait_ge(scores_for_exp, NU * g + u + 1)
                    if u == 0 and (not isinstance(g, int) or g >= 2):
                        act.wait_ge(pv_done, g - 1)
                    act.activation(p_view(par, kb)[:, h0:h0 + heads, :], t_view(u, (2 * u + 1) % 3), ACT.Exp,
                                   scale=SCALE).then_inc(exp_done, 1)
                    if u == 1 and maxrows:
                        copy_mT(g + 1, 1 - par)
                    if u == 2 and end is not None and k == 3:
                        copy_x1(end)
                    if u == (1 if k == 2 and end is not None else 2) and pv:
                        copy_pv(g - 1)
                    if u == 3 and end is not None and k == 2:
                        copy_yT(end)
                    if u == 3 and end is not None and k == 3:
                        copy_scores(end)
                    if u == 5 and end is not None and k == 3:
                        exp_gap(end)

            copy_mT(0, 0)
            for b in range(2):
                for s in range(2):
                    act.wait_ge(parts_stored[s][b], 16 * PARTS)
            act.wait_ge(ksplit, B)
            act.wait_ge(v_full, B)
            step(0, 2, pv=False)
            step(1, 3)
            with act.Fori(0, B - 1) as b:
                for k in range(4):
                    step(4 * b + 2 + k, k, end=b)
            step(G - 2, 0)
            step(G - 1, 1, maxrows=False)
            copy_pv(G - 1)
            copy_yT(B - 1)
            copy_x1(B - 1)
            copy_scores(B - 1)
            exp_gap(B - 1)
            act.wait_ge(fills_ready, 1)
            for e in range(1, E, 2):
                at = act.value_load(fill_row[0:1, e:e + 1], min_val=e * REGION, max_val=e * REGION + TOKENS)
                act.dma_start(rows_scratch[bass.ds(at, 2 * P), :].rearrange("(p a) c -> p (a c)", a=2),
                              fill[:, :, :].rearrange("p a c -> p (a c)")).then_inc(filled, 16)

            def silu(s, two):
                act.wait_ge(gate_full, s + 1)
                if not isinstance(s, int) or s >= 2:
                    act.wait_ge(h_ready, s - 1)
                act.activation(sg[:, two, :], slot[two][:, 0:F], ACT.Silu).then_inc(silu_done, 1)

            def weigh(j, ring, freed):
                act.wait_ge(y_full, j + 1)
                if freed is not None:
                    act.wait_ge(y_scattered[(ring - OUT_RING) % RING], freed)
                act.activation(ys[:, ring % OUT_RING, :], pvo[:, 0:C], ACT.Copy, scale=xg[:, ring, C + 1:C + 2]).then_inc(ys_ready, 1)

            def expert_step(s, m):
                if not isinstance(s, int) or s < ET:
                    silu(s, m % 2)
                if not isinstance(s, int) or s >= 2:
                    j = s - 2
                    ring = (m - 2) % RING
                    if isinstance(s, int):
                        freed = 16 * ((j - OUT_RING) // RING + 1) if j >= OUT_RING else None
                    else:
                        freed = 16 * ((j - OUT_RING - (ring - OUT_RING) % RING) // RING + 1)
                    weigh(j, ring, freed)

            expert_steps(act, expert_step)
            for b in range(B):
                act.wait_ge(shift_ready, b + 1)
                for t in range(TB if b < B - 1 else TB // 2):
                    tile = X[:, b * TB + t, :]
                    last = act.activation(tile, tile, ACT.Identity, bias=shift2[:, b, t:t + 1], scale=rstd2[:, b, t:t + 1])
                last.then_inc(norm2, 1)

        @block.vector
        def _(dve):
            chain, loop = [0], [None]
            LINKS = 11

            def link(instruction, carried=False):
                instruction.then_inc(dchain, 1)
                chain[0] += 1
                if loop[0] is None:
                    dve.wait_ge(dchain, chain[0])
                else:
                    dve.wait_ge(dchain, loop[0] * LINKS + chain[0])
                    if carried:
                        dve.sem_inc(dve_passed, 1)

            dve.memset(blank_k[:, :, :].rearrange("p a t -> p (a t)").bitcast(F32), 0.0)
            dve.memset(blank_q[:, :].bitcast(F32), 0.0).then_inc(blanks_ready, 1)
            dve.wait_ge(blanks_ready, 1)
            for a in range(2):
                last = dve.memset(blank_k[HALF * a:HALF * a + PARTS, a, :], 1.0)
            last.then_inc(blanks_ready, 1)
            dve.wait_ge(blanks_ready, 2)

            def blank(b):
                for c in range(2):
                    dve.tensor_copy(Ks[:, QPB * b:QPB * (b + 1), 2 * c:2 * c + 2, :].rearrange("p g h t -> p g (h t)"),
                                    blank_k[:, :, :].rearrange("p (o a) t -> p o (a t)", o=1).broadcast_to([P, QPB, 2 * T]))
                dve.tensor_copy(Qs[:, QPB * b:QPB * (b + 1)].rearrange("p g c t -> p (g c) t"),
                                blank_q[:, :].rearrange("p (o t) -> p o t", o=1).broadcast_to([P, 2 * QPB, T])).then_inc(blanked[b], 1)

            blank(0)
            dve.memset(pvo[:, :], 0.0)
            dve.memset(V9[:, :, :, :, D:D + 1], 1.0)
            dve.wait_ge(weights_full, 1)
            dve.tensor_scalar(lbT[:, :, :].rearrange("r j p -> r (j p)"), slot[1][0:LORA_R, 0:T], LORA_SCALE, None,
                              ALU.mult).then_inc(weights_out, 1)
            dve.wait_ge(weights_full, 2)
            dve.tensor_copy(WT[:, :, :].rearrange("p j c -> p (j c)"), slot[2][:, 0:3 * C]).then_inc(weights_out, 1)
            blank(1)
            for b in range(B):
                for s, ready, split in ((0, q_out, qsplit), (1, k_out, ksplit)):
                    high, mid, low = (parts[b][:, s, e, :] for e in range(PARTS))
                    dve.wait_ge(ready, 2 * (b + 1))
                    dve.tensor_tensor(rest[:, s, :], qk[:, s, :], high, ALU.subtract).then_inc(split_chain, 1)
                    dve.wait_ge(split_chain, 4 * b + 2 * s + 1)
                    dve.tensor_copy(mid, rest[:, s, :]).then_inc(split_chain, 1)
                    dve.wait_ge(split_chain, 4 * b + 2 * s + 2)
                    dve.tensor_tensor(low, rest[:, s, :], mid, ALU.subtract).then_inc(split, 1)
                dve.wait_ge(v_full, b + 1)
                if b == 0:
                    dve.wait_ge(late_loaded, 16 * LATE_DMAS)
                for t in range(TB):
                    last = dve.tensor_tensor(V9[:, QPB * b:QPB * (b + 1), t, :, 0:D],
                                             slot[1][:, T + t * C:T + (t + 1) * C].rearrange("p (i h d) -> p i h d", i=QPB, h=HQ),
                                             bv_rows[:, :].rearrange("p (i h d) -> p i h d", i=QPB, h=HQ), ALU.add)
                last.then_inc(v_out, 1)
                if b == 0:
                    dve.wait_ge(weights_full, 3)
                    dve.tensor_copy(WPT[:, :], slot[1][:, 0:C]).then_inc(weights_out, 1)

            def row_max(g, par, u, n):
                qb, h0, heads = S_UNITS[u]
                dve.wait_ge(scores_for_max, NU * g + u + 1)
                if u == 0 and (not isinstance(g, int) or g >= 2):
                    dve.wait_ge(mparts_ready, g - 1)
                dve.tensor_reduce(negm[:, par, qb, h0:h0 + heads], s_view(u, n), AX_X, ALU.max,
                                  negate=True).then_inc(max_done, 1)

            def normalize(g, i):
                dve.wait_ge(yT_full, g + 1)
                v = misc[:, :].rearrange("p (t h e) -> p t h e", t=TB, h=HQ)
                dve.reciprocal(rl[:, :, :], v[:, :, :, D]).then_inc(rl_ready, 1)
                dve.wait_ge(rl_ready, g + 1)
                dve.tensor_tensor(Y[:, :, i * HQ * D:(i + 1) * HQ * D].rearrange("p t (h d) -> p t h d", h=HQ), v[:, :, :, 0:D],
                                  rl[:, :, :].rearrange("p t (h a) -> p t h a", a=1).broadcast_to([P, TB, HQ, D]),
                                  ALU.mult).then_inc(y_done, 1)

            def statistics(src, mean_variance):
                for t in range(TB):
                    last = dve.bn_stats(stats[:, t, :], src[:, t, :])
                link(last, carried=True)
                for t in range(TB):
                    last = dve.bn_aggr(mean_variance[:, t, :], stats[:, t, :])
                last.then_inc(stats_ready, 1)

            def residual(b):
                dve.wait_ge(proj_full, b + 1)
                link(dve.tensor_tensor(XR[:, :, :].rearrange("p t c -> p (t c)"), misc[:, :],
                                       X[:, bass.ds(b * TB, TB), :].rearrange("p t c -> p (t c)"), ALU.add))
                statistics(XR, mv)

            def normed(b):
                dve.wait_ge(rstd_ready, b + 1)
                dve.wait_ge(scattered, 16 + 2 * TB * 16 * b)
                for t in range(TB):
                    last = dve.tensor_scalar(rows[:, 0, t, 0:C], XR[:, t, :], mv[:, t, 0:1], rstd[:, t:t + 1],
                                             ALU.subtract, ALU.mult)
                last.then_inc(x1_ready, 1)

            def choose(b):
                dve.wait_ge(scores_copied, b + 1)
                if not isinstance(b, int):
                    dve.sem_inc(dve_passed, 1)
                for t in range(TB):
                    last = dve.max(top[:, t, :], sc[:, t, :])
                link(last, carried=True)
                for t in range(TB):
                    last = dve.max_index(topi[:, t, :], top[:, t, :], sc[:, t, :])
                dve.tensor_tensor(gap[:, :], top[:, :, 1], top[:, :, 0], ALU.subtract).then_inc(gap_ready, 1)
                link(last)
                link(dve.tensor_copy(topf[:, :, :].rearrange("p j t -> p t j"), topi[:, :, 0:2]))
                for j in range(2):
                    last = dve.tensor_tensor(hot[:, j], lanes[:, :, :],
                                             topf[:, j, :].rearrange("p (t a) -> p t a", a=1).broadcast_to([P, TB, E]), ALU.is_equal)
                link(last)
                link(dve.tensor_tensor(hots[:, :, :], hot[:, 0], hot[:, 1], ALU.add))
                with nc.allow_low_precision(reason="counts up to four are exact in bf16"):
                    dve.tensor_reduce(hot_sum[:, :], hots[:, :, :].rearrange("p t e -> p e t"), AX_X, ALU.add).then_inc(hot_ready, 1)

            def place_rows(b):
                dve.wait_ge(egap_ready, b + 1)
                link(dve.tensor_scalar(gap[:, :], egap[:, :], 1.0, None, ALU.add))
                link(dve.reciprocal(gap[:, :], gap[:, :]))
                dve.tensor_copy(rows[:, 0, :, C + 1], gap[:, :])
                dve.tensor_tensor(rows[:, 1, :, C + 1], gap[:, :], egap[:, :], ALU.mult)
                dve.wait_ge(prefix_full, b + 1)
                for j in range(2):
                    last = dve.tensor_tensor(ranks[:, j], hot[:, j], misc[:, 0:TB * E].rearrange("p (t e) -> p t e", e=E), ALU.mult)
                link(last)
                if isinstance(b, int):
                    dve.tensor_copy(count[:, :], misc[:, TB * E:TB * E + E])
                link(dve.tensor_reduce(rank[:, :, :], ranks[:, :, :, :], AX_X, ALU.add))
                dve.tensor_tensor(carry[:, :], carry[:, :], hot_sum[:, :], ALU.add)
                dve.scalar_tensor_tensor(out=place[:, :, :], in0=topf[:, :, :], scalar=float(REGION), in1=rank[:, :, :],
                                         op0=ALU.mult, op1=ALU.add).then_inc(place_ready, 1)

            def step(g, k, end=None, scores=True, pv=True):
                par = k % 2
                for u in range(NU):
                    if scores:
                        row_max(g + 2, par, u, (2 * u) % 3)
                    if end is not None and k == 3:
                        if u == 1:
                            normed(end)
                        if u == 4:
                            choose(end)
                    if u == (2 if k == 2 and end is not None else 4) and pv:
                        normalize(g - 1, (k + 1) % 4)
                    if end is not None and k == 2 and u == 5:
                        residual(end)
                    if end is not None and k == 3 and u == 5:
                        place_rows(end)

            for g in range(2):
                for u in range(NU):
                    row_max(g, g, u, (NU * g + u) % 3)
            step(0, 2, pv=False)
            for s in range(2):
                dve.wait_ge(parts_stored[s][B - 1], 16 * PARTS)
            step(1, 3)
            dve.wait_ge(xb_ready, 1)
            dve.wait_ge(lists_ready, 1)
            with dve.Fori(0, B - 1) as b:
                loop[0] = b
                chain[0] = 0
                for k in range(4):
                    step(4 * b + 2 + k, k, end=b)
                assert chain[0] == LINKS, chain[0]
            loop[0] = None
            chain[0] = LINKS * (B - 1)
            step(G - 2, 0, scores=False)
            step(G - 1, 1, scores=False)
            normalize(G - 1, 3)
            residual(B - 1)
            normed(B - 1)
            choose(B - 1)
            place_rows(B - 1)

            link(dve.tensor_tensor(fill_f[:, :], count[:, :], region_f[:, :], ALU.add))
            dve.tensor_copy(fill_row[:, :], fill_f[:, :]).then_inc(fills_ready, 1)
            link(dve.tensor_tensor(over[:, :, :], count[:, :].rearrange("p (e a) -> p e a", a=1).broadcast_to([P, E, MAX_TILES]),
                                   steps16[:, :, :], ALU.is_gt))
            link(dve.tensor_reduce(ntiles[:, :], over[:, :, :], AX_X, ALU.add))
            link(dve.tensor_tensor(prod8[:, :, :], lower[:, :, :], ntiles[:, :].rearrange("p (a e) -> p a e", a=1).broadcast_to([P, E, E]), ALU.mult))
            link(dve.tensor_reduce(ends[:, :], prod8[:, :, :], AX_X, ALU.add))
            link(dve.tensor_tensor(past[:, :, :], tile_no[:, :, :], ends[:, :].rearrange("p (a e) -> p a e", a=1).broadcast_to([P, ET, E]), ALU.is_ge))
            link(dve.tensor_tensor(pastn[:, :, :], past[:, :, :], ntiles[:, :].rearrange("p (a e) -> p a e", a=1).broadcast_to([P, ET, E]), ALU.mult))
            dve.tensor_reduce(expert_f[:, :], past[:, :, :], AX_X, ALU.add)
            link(dve.tensor_reduce(first_f[:, :], pastn[:, :, :], AX_X, ALU.add))
            link(dve.tensor_tensor(first_f[:, :], tile_no[:, :, 0], first_f[:, :], ALU.subtract))
            link(dve.tensor_scalar(behind[:, :], first_f[:, :], -1.0, ntiles[:, E - 1:E], ALU.mult, ALU.add))
            link(dve.tensor_tensor(behind[:, :], behind[:, :], past[:, :, E - 1], ALU.mult))
            link(dve.tensor_tensor(first_f[:, :], first_f[:, :], behind[:, :], ALU.add))
            link(dve.tensor_scalar(expert_f[:, :], expert_f[:, :], float(E - 1), None, ALU.min))
            link(dve.tensor_scalar(first_f[:, :], first_f[:, :], float(P), None, ALU.mult))
            dve.tensor_copy(expert_of[:, :], expert_f[:, :])
            dve.scalar_tensor_tensor(out=row_of[:, :], in0=expert_f[:, :], scalar=float(REGION), in1=first_f[:, :],
                                     op0=ALU.mult, op1=ALU.add).then_inc(tables_ready, 1)

            def copy_xT(j, two):
                dve.wait_ge(xgT_full, j + 1)
                if not isinstance(j, int) or j >= 2:
                    dve.wait_ge(gu_full, j - 1)
                dve.tensor_copy(xgT[:, two, :], misc[:, 0:P]).then_inc(xgT_ready, 1)

            def copy_hT(j, two):
                dve.wait_ge(hT_full, j + 1)
                if not isinstance(j, int) or j >= 2:
                    dve.wait_ge(y_full, j - 1)
                src = slot[2][:, two * T:two * T + NFC * P]
                dve.tensor_copy(hT[:, two, 0:NFC - 1].rearrange("p k t -> p (k t)"), src[:, 0:(NFC - 1) * P])
                dve.tensor_copy(hT[0:FC[-1][1], two, NFC - 1, :], src[0:FC[-1][1], (NFC - 1) * P:NFC * P]).then_inc(hT_ready, 1)

            def hidden(s, two):
                dve.wait_ge(silu_done, s + 1)
                dve.wait_ge(gu_full, s + 1)
                dve.tensor_tensor(hid[:, two, :], slot[two][:, T:T + F], sg[:, two, :], ALU.mult).then_inc(h_ready, 1)

            def expert_step(s, m):
                static = isinstance(s, int)
                if not static or s + 1 < ET:
                    copy_xT(s + 1, (m + 1) % 2)
                if not static or 1 <= s <= ET:
                    copy_hT(s - 1, (m - 1) % 2)
                if not static or s < ET:
                    hidden(s, m % 2)

            copy_xT(0, 0)
            expert_steps(dve, expert_step)

            def shift(b):
                dve.wait_ge(rstd_ready, B + b + 1)
                dve.scalar_tensor_tensor(out=shift2[:, b], in0=mv2[:, b, :, 0], scalar=-1.0, in1=rstd2[:, b],
                                         op0=ALU.mult, op1=ALU.mult).then_inc(shift_ready, 1)

            for b in range(B):
                xb = X[:, b * TB:(b + 1) * TB, :].rearrange("p t c -> p (t c)")
                if b in POOL_ADDS:
                    dve.wait_ge(first_added, POOL_ADDS.index(b) + 1)
                else:
                    dve.wait_ge(back_loaded[b], 32)
                    link(dve.tensor_tensor(xb, xb, back[:, b, 0].rearrange("p t c -> p (t c)"), ALU.add))
                link(dve.tensor_tensor(xb, xb, back[:, b, 1].rearrange("p t c -> p (t c)"), ALU.add))
                statistics(X[:, b * TB:(b + 1) * TB, :], mv2[:, b])
                if b:
                    shift(b - 1)
            shift(B - 1)
            for t in range(TB // 2, TB):
                tile = X[:, (B - 1) * TB + t, :]
                last = dve.tensor_scalar(tile, tile, mv2[:, B - 1, t, 0:1], rstd2[:, B - 1, t:t + 1], ALU.subtract, ALU.mult)
            last.then_inc(last_half, 1)

        @block.tensor
        def _(pe):
            def transpose_x(b):
                pe.wait_ge(x_loaded[b], 16)
                if b:
                    pe.wait_ge(xT_out, b)
                for t in range(TB):
                    last = pe.transpose(misc[:, t * P:(t + 1) * P], X[:, b * TB + t, :], identf[:, :])
                last.then_inc(xT_full, 1)

            pe.wait_ge(ident_ready, 1)
            transpose_x(0)
            pe.wait_ge(lb_loaded, 32)
            for j in range(4):
                last = pe.transpose(slot[1][0:LORA_R, j * P:(j + 1) * P], LB[:, j, :], identf[:, :])
            last.then_inc(weights_full, 1)
            pe.wait_ge(w_loaded, 16 * W_DMAS)
            for j in range(3):
                pe.matmul(slot[2][:, j * C:(j + 1) * C], WA[:, j, :], identf[:, :], start=(j == 0), stop=False, skip_group_check=True)
            pe.wait_ge(weights_out, 1)
            pe.matmul(slot[2][:, 0:3 * C], LA[:, 0, :], lbT[:, 0:3, :].rearrange("r j p -> r (j p)"), start=False, stop=True,
                      skip_group_check=True).then_inc(weights_full, 1)
            for b in range(B):
                pe.wait_ge(xT_out, b + 1)
                if b == 0:
                    pe.wait_ge(weights_out, 2)
                for j, full, done in ((0, q_full, q_out), (1, k_full, k_out)):
                    if b >= 2:
                        pe.wait_ge(done, 2 * (b - 1))
                    pe.matmul(slot[2 * (b % 2)][:, j * T:(j + 1) * T], WT[:, j, :], xT[:, b % 2, :], start=True, stop=True).then_inc(full, 1)
                if b + 1 < B:
                    transpose_x(b + 1)
                if b:
                    pe.wait_ge(v_out, b)
                for t in range(TB):
                    last = pe.matmul(slot[1][:, T + t * C:T + (t + 1) * C], xT[:, b % 2, t * P:(t + 1) * P], WT[:, 2, :], start=True, stop=True)
                last.then_inc(v_full, 1)
                if b == 0:
                    pe.wait_ge(late_loaded, 16 * LATE_DMAS)
                    pe.matmul(slot[1][:, 0:C], WP[:, :], identf[:, :], start=True, stop=False, skip_group_check=True)
                    pe.matmul(slot[1][:, 0:C], LA[:, 1, :], lbT[:, 3, :], start=False, stop=True, skip_group_check=True).then_inc(weights_full, 1)

            def scores_q(g, u, n):
                qb, h0, heads = S_UNITS[u]
                v = s_view(u, n)
                per_bank = {3: 1, 2: 1, 1: 2, 0: 4}[qb]
                for h in range(0, heads, per_bank):
                    pe.matmul(v[:, h:h + per_bank, qb * P:(qb + 1) * P], identb[:, :], maskb[:, 0:per_bank, :],
                              start=True, stop=False, skip_group_check=True)
                    for j in range(h, h + per_bank):
                        head = h0 + j
                        last = pe.matmul(v[:, j, :], Qs[:, bass.ds(g, 1), head // 2, qb * P:(qb + 1) * P],
                                         Ks[:, bass.ds(g, 1), head, 0:(qb + 1) * P],
                                         start=False, stop=True, skip_group_check=True)
                last.then_inc(scores_for_max, 1)

            def scores_k(g, u, n, masked):
                kb, h0, heads = T_UNITS[u]
                v = t_view(u, n)
                if masked:
                    per_bank = {0: 1, 1: 1, 2: 2, 3: 4}[kb]
                    for h in range(0, heads, per_bank):
                        pe.matmul(v[:, h:h + per_bank, 0:P], identb[:, :], mask_after[:, 0:per_bank, :],
                                  start=True, stop=False, skip_group_check=True)
                for j in range(heads):
                    head = h0 + j
                    last = pe.matmul(v[:, j, :], Ks[:, bass.ds(g, 1), head, kb * P:(kb + 1) * P],
                                     Qs[:, bass.ds(g, 1), head // 2, kb * P:T], start=not masked, stop=True,
                                     skip_group_check=masked)
                last.then_inc(scores_for_exp, 1)

            def transpose_max(g, par):
                pe.wait_ge(mparts_ready, g + 1)
                for t in range(TB):
                    last = pe.transpose(miscb[0:HQ * PARTS, t * P:(t + 1) * P],
                                        mparts[:, par, t].rearrange("p h e -> p (h e)"), identb[:, :])
                last.then_inc(mT_full, 1)

            def weighted_values(g, par, kb):
                if isinstance(g, int) and g >= MASKED_FROM:
                    pe.wait_ge(exp_done, NU * g + [2, 4, 5, 6][kb])
                else:
                    pe.wait_ge(selected, TB * g + kb + 1)
                if kb == 0:
                    pe.wait_ge(vst_ready, g + 1)
                    pe.wait_ge(pvs_copied, g)
                for h in range(HQ):
                    last = pe.matmul(pvo[32 * h:32 * h + D + 1, kb * P:T], vst[:, par, kb, h, :], p_view(par, kb)[:, h, :],
                                     start=(kb == 0), stop=(kb == TB - 1))
                if kb == TB - 1:
                    last.then_inc(pv_done, 1)

            def transpose_pv(g):
                pe.wait_ge(pvs_copied, g + 1)
                for t in range(TB):
                    last = pe.transpose(misc[:, t * P:(t + 1) * P], pvs[:, t * P:(t + 1) * P], identf[:, :])
                last.then_inc(yT_full, 1)

            def transpose_y(b):
                pe.wait_ge(y_done, QPB * b + QPB)
                for t in range(TB):
                    last = pe.transpose(misc[:, t * P:(t + 1) * P], Y[:, t, :], identf[:, :])
                last.then_inc(fT_full, 1)

            def project(b):
                pe.wait_ge(fT_out, b + 1)
                for t in range(TB):
                    last = pe.matmul(misc[:, t * C:(t + 1) * C], yT[:, t * P:(t + 1) * P], WPT[:, :], start=True, stop=True)
                last.then_inc(proj_full, 1)

            def transpose_x1(b):
                pe.wait_ge(x1_ready, b + 1)
                for t in range(TB):
                    last = pe.transpose(misc[:, t * P:(t + 1) * P], rows[:, 0, t, 0:C], identf[:, :])
                last.then_inc(x1T_full, 1)

            def route(b):
                pe.wait_ge(x1T_out, b + 1)
                for t in range(TB):
                    last = pe.matmul(misc[:, t * E:(t + 1) * E], x1T[:, t * P:(t + 1) * P], RW[:, :], start=True, stop=True)
                last.then_inc(router_full, 1)

            def count_before(b):
                pe.wait_ge(hot_ready, b + 1)
                pe.matmul(misc[:, 0:TB * E], before[:, :], hots[:, :, :].rearrange("p t e -> p (t e)"), start=True, stop=False, skip_group_check=True)
                for t in range(TB - 1):
                    n = TB - 1 - t
                    pe.matmul(misc[:, (t + 1) * E:TB * E].rearrange("p (t e) -> p t e", e=E), onesb[:, :],
                              hots[:, t:t + 1, :].broadcast_to([P, n, E]), start=False, stop=False, skip_group_check=True)
                pe.matmul(misc[:, 0:TB * E].rearrange("p (t e) -> p t e", e=E), onesb[:, :],
                          carry[:, :].rearrange("p (a e) -> p a e", a=1).broadcast_to([P, TB, E]), start=False, stop=False, skip_group_check=True)
                pe.matmul(misc[:, TB * E:TB * E + E], onesb[:, :], carry[:, :], start=False, stop=False, skip_group_check=True)
                pe.matmul(misc[:, TB * E:TB * E + E], onesb[:, :], hot_sum[:, :], start=False, stop=True,
                          skip_group_check=True).then_inc(prefix_full, 1)

            def step(g, k, end=None, scores=True, maxrows_=True):
                static = isinstance(g, int)
                first = static and g == 0
                par = k % 2
                last4 = end is not None
                for u in range(NU):
                    if scores:
                        if first:
                            pe.wait_ge(max_done, NU * 2)
                        if not first or u >= 2:
                            pe.wait_ge(exp_done, NU * g + u - 1)
                        scores_q(g + 2, u, (2 * u) % 3)
                    if u == NU - 1:
                        weighted_values(g, par, 0)
                    if u == 0:
                        pe.wait_ge(maxrows[par], 32 * (g - par) + 64)
                    if scores:
                        pe.wait_ge(max_done, NU * g + 2 * NU + u)
                    else:
                        pe.wait_ge(max_done, NU * G)
                        pe.wait_ge(exp_done, NU * g + u - 2)
                    scores_k(g, u, (2 * u + 1) % 3, masked=not scores)
                    if not first:
                        for kb in range(1, TB):
                            if u == PV_AT[k == 2 and last4][kb - 1]:
                                weighted_values(g - 1, 1 - par, kb)
                    if u == (1 if scores else 0) and maxrows_:
                        if static and g <= 1:
                            pe.wait_ge(mT_copied, g + 1)
                        else:
                            pe.wait_ge(y_done, g - 1)
                            if k == 0 and not scores:
                                pe.wait_ge(place_ready, B - 1)
                            if k == 3 and last4:
                                pe.wait_ge(stats_ready, end + 1)
                        transpose_max(g + 1, 1 - par)
                    if u == 2 and last4 and k == 3:
                        pe.wait_ge(mT_copied, g + 2)
                        transpose_x1(end)
                    if u == 3 and last4 and k == 3:
                        route(end)
                    if u == 4 and last4 and k == 3:
                        pe.wait_ge(scores_copied, end + 1)
                        transpose_pv(g - 1)
                    if u == (2 if k == 2 and last4 else 3) and not first and not (last4 and k == 3):
                        if maxrows_:
                            pe.wait_ge(mT_copied, g + 2)
                        else:
                            pe.wait_ge(y_done, g - 1)
                        transpose_pv(g - 1)
                    if u == 3 and last4 and k == 2:
                        transpose_y(end)
                    if u == 4 and last4 and k == 2:
                        project(end)
                    if u == 5 and last4 and k == 3:
                        pe.wait_ge(y_done, g)
                        count_before(end)

            pe.wait_ge(consts_ready, 2)
            pe.wait_ge(stacks_loaded, STACK_DMAS)
            for g in range(2):
                for u in range(NU):
                    n = NU * g + u
                    if n >= 3:
                        pe.wait_ge(max_done, n - 2)
                    elif n == 0:
                        pe.wait_ge(k_out, 2 * (B - 1))
                    elif n == 1:
                        pe.wait_ge(v_out, B)
                    else:
                        pe.wait_ge(k_out, 2 * B)
                    scores_q(g, u, n % 3)
                    if n == NU + 2:
                        pe.wait_ge(xT_out, B)
                        transpose_max(0, 0)
            step(0, 2)
            step(1, 3)
            pe.wait_ge(lists_ready, 1)
            with pe.Fori(0, B - 1) as b:
                pe.wait_ge(stacks_loaded, STACK_DMAS * b + 2 * STACK_DMAS)
                for k in range(4):
                    step(4 * b + 2 + k, k, end=b)
            pe.wait_ge(mask_ready, 1)
            step(G - 2, 0, scores=False)
            step(G - 1, 1, scores=False, maxrows_=False)
            for kb in range(1, TB):
                weighted_values(G - 1, 1, kb)
            pe.wait_ge(y_done, G - 1)
            transpose_pv(G - 1)
            transpose_y(B - 1)
            project(B - 1)
            pe.wait_ge(stats_ready, B)
            transpose_x1(B - 1)
            route(B - 1)
            pe.wait_ge(scores_copied, B)
            count_before(B - 1)

            def transpose_rows(j, ring):
                if isinstance(j, int):
                    pe.wait_ge(xg_loaded[ring], 16 * (j // RING + 1))
                else:
                    pe.wait_ge(xg_loaded[ring], 16 * ((j - ring) // RING + 1))
                if not isinstance(j, int) or j >= 1:
                    pe.wait_ge(xgT_ready, j)
                pe.transpose(misc[:, 0:P], xg[:, ring, 0:C], identf[:, :]).then_inc(xgT_full, 1)

            def gate_up(s, two, e):
                pe.wait_ge(xgT_ready, s + 1)
                if not isinstance(s, int) or s >= 2:
                    pe.wait_ge(h_ready, s - 1)
                for w, full in enumerate((gate_full, gu_full)):
                    pe.matmul(slot[two][:, w * T:w * T + F], xgT[:, two, :],
                              GUW[:, bass.ds(e, 1), w, :].rearrange("p e f -> p (e f)"), start=True, stop=True).then_inc(full, 1)

            def transpose_hidden(j, two):
                pe.wait_ge(h_ready, j + 1)
                for k, (f0, fn) in enumerate(FC):
                    last = pe.transpose(slot[2][0:fn, two * T + k * P:two * T + (k + 1) * P], hid[:, two, f0:f0 + fn], identf[:, :])
                last.then_inc(hT_full, 1)

            def down(j, two, e):
                pe.wait_ge(hT_ready, j + 1)
                if not isinstance(j, int) or j >= 1:
                    pe.wait_ge(ys_ready, j)
                for k, (f0, fn) in enumerate(FC):
                    last = pe.matmul(pvo[:, 0:C], hT[0:fn, two, k, :], DW[0:fn, bass.ds(e, 1), k, :].rearrange("p e c -> p (e c)"),
                                     start=(k == 0), stop=(k == NFC - 1))
                last.then_inc(y_full, 1)

            def expert_number(j):
                return pe.value_load(expert_of[0:1, bass.ds(j, 1)], min_val=0, max_val=E - 1)

            experts = {}

            def expert_step(s, m):
                static = isinstance(s, int)
                if (s == 0 or s == LOOP_ENDS) if static else m == LOOP_FROM % RING:
                    experts.clear()
                    experts[m] = expert_number(s)
                if not static or s + 1 < ET:
                    transpose_rows(s + 1, (m + 1) % RING)
                if not static or s < ET:
                    gate_up(s, m % 2, experts[m])
                ends_body = s == LOOP_FROM - 1 or s >= ET - 1 if static else m == (LOOP_FROM - 1) % RING
                if not ends_body:
                    experts[(m + 1) % RING] = expert_number(s + 1)
                if not static or 1 <= s <= ET:
                    transpose_hidden(s - 1, (m - 1) % 2)
                if not static or s >= 2:
                    if (m - 2) % RING not in experts:
                        experts[(m - 2) % RING] = expert_number(s - 2)
                    down(s - 2, m % 2, experts[(m - 2) % RING])

            pe.wait_ge(tables_ready, 1)
            pe.wait_ge(experts_loaded, 16 * (2 + NFC))
            pe.wait_ge(exp_done, NU * G)
            pe.wait_ge(place_ready, B)
            transpose_rows(0, 0)
            expert_steps(pe, expert_step)


_INS = ['L0_attn_x', 'L0_attn_w_attn', 'L0_attn_b_attn', 'L0_attn_la_attn', 'L0_attn_lb_attn', 'L0_attn_w_proj',
        'L0_attn_b_proj', 'L0_attn_la_proj', 'L0_attn_lb_proj', 'L0_ffn_router_w', 'L0_ffn_gate_proj',
        'L0_ffn_up_proj', 'L0_ffn_down_proj']
_OUTS = [((4, 512, 128), 'float32')]


def kernel(**inputs):
    import numpy as _np
    import concourse.bacc as _bacc
    from concourse import mybir as _mybir
    from concourse.bass_utils import run_bass_kernel_spmd as _run

    nc = _bacc.Bacc("TRN2", target_bir_lowering=False, num_devices=1)
    arrays, args = {}, []
    for name in _INS:
        a = _np.ascontiguousarray(inputs[name])
        arrays[f"in_{name}_dram"] = a
        args.append(nc.dram_tensor(f"in_{name}_dram", a.shape, _mybir.dt.from_np(a.dtype), kind="ExternalInput").ap())
    for i, (shape, dtype) in enumerate(_OUTS):
        dt = _mybir.dt.from_np(_np.dtype(dtype))
        args.append(nc.dram_tensor(f"out_{i}_dram", shape, dt, kind="ExternalOutput").ap())
    args.append(nc.dram_tensor("parts_scratch", (4, 2, 128 * 6, 512), _mybir.dt.bfloat16).ap())
    args.append(nc.dram_tensor("rows_scratch", (8 * (2048 + 256), 130), _mybir.dt.float32).ap())
    args.append(nc.dram_tensor("chosen_scratch", (2 * 2048, 128), _mybir.dt.float32).ap())
    causal_attention_then_top2_experts(nc, *args)
    r = _run(nc, [arrays], core_ids=[0])
    return r.results[0]["out_0_dram"]
```
